# Optimizing a Trainium2 kernel written in Bass

```python
import numpy as np
import jax
import jax.numpy as jnp

def _softmax(x, axis=-1):
    return jax.nn.softmax(x, axis=axis)

def _gelu(x):
    return jax.nn.gelu(x, approximate=True)

def _silu(x):
    return jax.nn.silu(x)

def _sigmoid(x):
    return jax.nn.sigmoid(x)

def _layernorm(x, axis=-1, eps=1e-05):
    m = jnp.mean(x, axis=axis, keepdims=True)
    v = jnp.var(x, axis=axis, keepdims=True)
    return (x - m) / jnp.sqrt(v + eps)

def _scatter_add(tgt, idx, src, axis=0):
    return tgt.at[idx].add(src)

def _segment_sum(src, seg, n):
    return jax.ops.segment_sum(src, seg, n)
kernel_name = 'mk_seq_postln_d2_jaxref_r8_c0bedb'

def setup_inputs(seed: int=0):
    np.random.seed(seed)
    _w = jnp.asarray

    def _L0_attn_setup():
        import jax, jax.numpy as jnp
        import numpy as np
        LN_EPS = 1e-05

        def _forward(x, W_in, conv_w, conv_b, a_param, W_out, ln_w, ln_b):
            B, T, D = x.shape
            K = conv_w.shape[-1]
            proj = jnp.einsum('btd,ed->bte', x, W_in)
            gate, val = (proj[..., :D], proj[..., D:])
            g = jax.nn.sigmoid(gate)
            v = jax.lax.conv_general_dilated(val.transpose(0, 2, 1), conv_w, window_strides=(1,), padding=[(K // 2, K // 2)], feature_group_count=D, dimension_numbers=('NCH', 'OIH', 'NCH'))
            v = (v + conv_b[None, :, None]).transpose(0, 2, 1)
            a = jnp.tanh(a_param)
            gv = g * v

            def step(h, u):
                h = a * h + u
                return (h, h)
            h0 = jnp.zeros((B, D), dtype=x.dtype)
            _, y = jax.lax.scan(step, h0, gv.transpose(1, 0, 2))
            y = y.transpose(1, 0, 2)
            res = x + jnp.einsum('btd,ed->bte', y, W_out)
            mu = jnp.mean(res, axis=-1, keepdims=True)
            var = jnp.mean(jnp.square(res - mu), axis=-1, keepdims=True)
            return (res - mu) * jax.lax.rsqrt(var + LN_EPS) * ln_w + ln_b
        key = jax.random.key(seed)
        ks = jax.random.split(key, 6)
        B, T, D, K = (8, 256, 128, 5)
        x = jax.random.normal(ks[0], (B, T, D), dtype=jnp.float32)
        W_in = jax.random.normal(ks[1], (2 * D, D), dtype=jnp.float32) * (1.0 / np.sqrt(D))
        conv_w = jax.random.normal(ks[2], (D, 1, K), dtype=jnp.float32) * (1.0 / np.sqrt(K))
        conv_b = jax.random.normal(ks[3], (D,), dtype=jnp.float32) * 0.1
        a_param = jax.random.normal(ks[4], (D,), dtype=jnp.float32)
        W_out = jax.random.normal(ks[5], (D, D), dtype=jnp.float32) * (1.0 / np.sqrt(D))
        ln_w = jnp.ones((D,), dtype=jnp.float32)
        ln_b = jnp.zeros((D,), dtype=jnp.float32)
        return {'x': x, 'W_in': W_in, 'conv_w': conv_w, 'conv_b': conv_b, 'a_param': a_param, 'W_out': W_out, 'ln_w': ln_w, 'ln_b': ln_b}
    _L0_attn_in = _L0_attn_setup()

    def _L0_ffn_setup():
        import jax, jax.numpy as jnp
        import numpy as np
        D_MODEL = 128
        D_FF = 512
        N_EXPERTS = 8
        INIT_SCALE = 0.1

        def _trunc_normal(key, shape, std):
            return std * jax.random.truncated_normal(key, -2.0, 2.0, shape, dtype=jnp.float32)
        key = jax.random.key(seed)
        ks = jax.random.split(key, 5)
        x = jax.random.normal(ks[0], (4, 128, D_MODEL), dtype=jnp.float32)
        router_W = _trunc_normal(ks[1], (D_MODEL, N_EXPERTS), INIT_SCALE / np.sqrt(D_MODEL))
        router_b = jnp.zeros((N_EXPERTS,), dtype=jnp.float32)
        W1 = _trunc_normal(ks[2], (N_EXPERTS, D_MODEL, D_FF), INIT_SCALE / np.sqrt(D_MODEL))
        b1 = jnp.zeros((N_EXPERTS, D_FF), dtype=jnp.float32)
        W2 = _trunc_normal(ks[3], (N_EXPERTS, D_FF, D_MODEL), INIT_SCALE / np.sqrt(D_FF))
        b2 = jnp.zeros((N_EXPERTS, D_MODEL), dtype=jnp.float32)
        return {'x': x, 'router_W': router_W, 'router_b': router_b, 'W1': W1, 'b1': b1, 'W2': W2, 'b2': b2}
    _L0_ffn_in = _L0_ffn_setup()

    def _L1_attn_setup():
        import jax, jax.numpy as jnp
        import numpy as np
        B, T, HID = (16, 64, 128)
        NH, NKV, D = (8, 4, 128)
        THETA = 10000.0

        def _rotate_half(x):
            x1, x2 = (x[..., :x.shape[-1] // 2], x[..., x.shape[-1] // 2:])
            return jnp.concatenate((-x2, x1), axis=-1)
        key = jax.random.key(seed)
        k0, k1, k2, k3, k4 = jax.random.split(key, 5)
        s = 0.02
        return {'hidden_states': jax.random.normal(k0, (B, T, HID), dtype=jnp.float32), 'Wq': s * jax.random.normal(k1, (HID, NH * D), dtype=jnp.float32), 'Wk': s * jax.random.normal(k2, (HID, NKV * D), dtype=jnp.float32), 'Wv': s * jax.random.normal(k3, (HID, NKV * D), dtype=jnp.float32), 'Wo': s * jax.random.normal(k4, (NH * D, HID), dtype=jnp.float32)}
    _L1_attn_in = _L1_attn_setup()

    def _L1_ffn_setup():
        import jax, jax.numpy as jnp
        import numpy as np
        DIM = 128
        DEPTH = 6
        HEADS = 16
        DIM_HEAD = 64
        WINDOW = 32
        INNER = HEADS * DIM_HEAD
        DIM_INNER = int(DIM * 4 * 2 / 3)
        QK_SCALE = 8.0

        def shift_tokens(t):
            a, s = jnp.split(t, 2, -1)
            s = jnp.pad(s, ((0, 0), (1, 0), (0, 0)))[:, :-1]
            return jnp.concatenate([a, s], -1)

        def l2norm(t):
            return t / jnp.maximum(jnp.linalg.norm(t, axis=-1, keepdims=True), 1e-12)

        def rotate_half(x):
            x1, x2 = jnp.split(x, 2, -1)
            return jnp.concatenate([-x2, x1], -1)

        def rotary_tables(n):
            half = jnp.arange(0, DIM_HEAD, 2, dtype=jnp.float32)
            inv_freq = 1.0 / 10000.0 ** (half / DIM_HEAD)
            t = jnp.arange(n, dtype=jnp.float32)
            freqs = t[:, None] * inv_freq[None, :]
            freqs = jnp.concatenate([freqs, freqs], -1)
            base_scale = (half + 0.4 * DIM_HEAD) / (1.4 * DIM_HEAD)
            power = (t - n // 2) / (WINDOW // 2)
            scale = base_scale[None, :] ** power[:, None]
            scale = jnp.concatenate([scale, scale], -1)
            return (freqs, scale)

        def local_attention(q, k, v):
            b, h, n, d = q.shape
            w = WINDOW
            nw = n // w
            bq = q.reshape(b, h, nw, w, d)
            bk = k.reshape(b, h, nw, w, d)
            bv = v.reshape(b, h, nw, w, d)

            def look(t):
                p = jnp.pad(t, ((0, 0), (0, 0), (1, 0), (0, 0), (0, 0)))
                return jnp.concatenate([p[:, :, :nw], p[:, :, 1:]], axis=3)
            bk2, bv2 = (look(bk), look(bv))
            seq = jnp.arange(n).reshape(nw, w)
            seq_p = jnp.pad(seq, ((1, 0), (0, 0)), constant_values=-1)
            jt = jnp.concatenate([seq_p[:nw], seq_p[1:]], axis=1)
            it = seq[:, :, None]
            jb = jt[:, None, :]
            mask = (it < jb) | (it > jb + w) | (jb == -1)
            sim = jnp.einsum('bhwie,bhwje->bhwij', bq, bk2) * QK_SCALE
            sim = jnp.where(mask, -jnp.finfo(sim.dtype).max, sim)
            attn = jax.nn.softmax(sim, -1)
            out = jnp.einsum('bhwij,bhwje->bhwie', attn, bv2)
            return out.reshape(b, h, n, d)

        def attn_layer(x, Wqkv, qs, ksc, Wo):
            b, n, _ = x.shape
            qkv = x @ Wqkv
            q, k, v = jnp.split(qkv, 3, -1)
            sh = lambda t: t.reshape(b, n, HEADS, DIM_HEAD).transpose(0, 2, 1, 3)
            q, k, v = (sh(q), sh(k), sh(v))
            q = l2norm(q) * qs
            k = l2norm(k) * ksc
            freqs, scale = rotary_tables(n)
            cos, sin = (jnp.cos(freqs), jnp.sin(freqs))
            q = q * cos * scale + rotate_half(q) * sin * scale
            inv = 1.0 / scale
            k = k * cos * inv + rotate_half(k) * sin * inv
            out = local_attention(q, k, v)
            out = out.transpose(0, 2, 1, 3).reshape(b, n, INNER)
            return out @ Wo

        def ffn_layer(x, g, bln, W1, b1, W2, b2):
            mu = x.mean(-1, keepdims=True)
            var = ((x - mu) ** 2).mean(-1, keepdims=True)
            xn = (x - mu) / jnp.sqrt(var + 1e-05) * g + bln
            hg = xn @ W1 + b1
            a, gate = jnp.split(hg, 2, -1)
            return a * jax.nn.gelu(gate, approximate=False) @ W2 + b2
        key = jax.random.key(seed)
        ks = jax.random.split(key, 8)
        B, N = (2, 256)
        init = lambda k, shape: jax.random.normal(k, shape, jnp.float32) * 0.02
        return {'x': jax.random.normal(ks[0], (B, N, DIM), jnp.float32), 'Wqkv': init(ks[1], (DEPTH, DIM, 3 * INNER)), 'q_scale': jnp.ones((DEPTH, DIM_HEAD), jnp.float32), 'k_scale': jnp.ones((DEPTH, DIM_HEAD), jnp.float32), 'Wo': init(ks[2], (DEPTH, INNER, DIM)), 'ln_g': jnp.ones((DEPTH, DIM), jnp.float32), 'ln_b': jnp.zeros((DEPTH, DIM), jnp.float32), 'W1': init(ks[3], (DEPTH, DIM, 2 * DIM_INNER)), 'b1': jnp.zeros((DEPTH, 2 * DIM_INNER), jnp.float32), 'W2': init(ks[4], (DEPTH, DIM_INNER, DIM)), 'b2': jnp.zeros((DEPTH, DIM), jnp.float32)}
    _L1_ffn_in = _L1_ffn_setup()
    _d = {'L0_attn_x': _L0_attn_in['x'], 'L0_attn_W_in': _L0_attn_in['W_in'], 'L0_attn_conv_w': _L0_attn_in['conv_w'], 'L0_attn_conv_b': _L0_attn_in['conv_b'], 'L0_attn_a_param': _L0_attn_in['a_param'], 'L0_attn_W_out': _L0_attn_in['W_out'], 'L0_attn_ln_w': _L0_attn_in['ln_w'], 'L0_attn_ln_b': _L0_attn_in['ln_b'], 'L0_ffn_router_W': _L0_ffn_in['router_W'], 'L0_ffn_router_b': _L0_ffn_in['router_b'], 'L0_ffn_W1': _L0_ffn_in['W1'], 'L0_ffn_b1': _L0_ffn_in['b1'], 'L0_ffn_W2': _L0_ffn_in['W2'], 'L0_ffn_b2': _L0_ffn_in['b2'], 'L1_attn_Wq': _L1_attn_in['Wq'], 'L1_attn_Wk': _L1_attn_in['Wk'], 'L1_attn_Wv': _L1_attn_in['Wv'], 'L1_attn_Wo': _L1_attn_in['Wo'], 'L1_ffn_Wqkv': _L1_ffn_in['Wqkv'], 'L1_ffn_q_scale': _L1_ffn_in['q_scale'], 'L1_ffn_k_scale': _L1_ffn_in['k_scale'], 'L1_ffn_Wo': _L1_ffn_in['Wo'], 'L1_ffn_ln_g': _L1_ffn_in['ln_g'], 'L1_ffn_ln_b': _L1_ffn_in['ln_b'], 'L1_ffn_W1': _L1_ffn_in['W1'], 'L1_ffn_b1': _L1_ffn_in['b1'], 'L1_ffn_W2': _L1_ffn_in['W2'], 'L1_ffn_b2': _L1_ffn_in['b2']}
    _x0 = _d['L0_attn_x']
    _d['L0_attn_x'] = jax.random.normal(jax.random.fold_in(jax.random.key(seed), 1), (4, 512, 128), dtype=_x0.dtype)
    del _x0
    return _d

def reference(L0_attn_x, L0_attn_W_in, L0_attn_conv_w, L0_attn_conv_b, L0_attn_a_param, L0_attn_W_out, L0_attn_ln_w, L0_attn_ln_b, L0_ffn_router_W, L0_ffn_router_b, L0_ffn_W1, L0_ffn_b1, L0_ffn_W2, L0_ffn_b2, L1_attn_Wq, L1_attn_Wk, L1_attn_Wv, L1_attn_Wo, L1_ffn_Wqkv, L1_ffn_q_scale, L1_ffn_k_scale, L1_ffn_Wo, L1_ffn_ln_g, L1_ffn_ln_b, L1_ffn_W1, L1_ffn_b1, L1_ffn_W2, L1_ffn_b2):

    def _L0_attn_ref(x, W_in, conv_w, conv_b, a_param, W_out, ln_w, ln_b):
        import jax, jax.numpy as jnp
        import numpy as np
        LN_EPS = 1e-05

        def _forward(x, W_in, conv_w, conv_b, a_param, W_out, ln_w, ln_b):
            B, T, D = x.shape
            K = conv_w.shape[-1]
            proj = jnp.einsum('btd,ed->bte', x, W_in)
            gate, val = (proj[..., :D], proj[..., D:])
            g = jax.nn.sigmoid(gate)
            v = jax.lax.conv_general_dilated(val.transpose(0, 2, 1), conv_w, window_strides=(1,), padding=[(K // 2, K // 2)], feature_group_count=D, dimension_numbers=('NCH', 'OIH', 'NCH'))
            v = (v + conv_b[None, :, None]).transpose(0, 2, 1)
            a = jnp.tanh(a_param)
            gv = g * v

            def step(h, u):
                h = a * h + u
                return (h, h)
            h0 = jnp.zeros((B, D), dtype=x.dtype)
            _, y = jax.lax.scan(step, h0, gv.transpose(1, 0, 2))
            y = y.transpose(1, 0, 2)
            res = x + jnp.einsum('btd,ed->bte', y, W_out)
            mu = jnp.mean(res, axis=-1, keepdims=True)
            var = jnp.mean(jnp.square(res - mu), axis=-1, keepdims=True)
            return (res - mu) * jax.lax.rsqrt(var + LN_EPS) * ln_w + ln_b
        return _forward(x, W_in, conv_w, conv_b, a_param, W_out, ln_w, ln_b)

    def _L0_ffn_ref(x, router_W, router_b, W1, b1, W2, b2):
        import jax, jax.numpy as jnp
        import numpy as np
        D_MODEL = 128
        D_FF = 512
        N_EXPERTS = 8
        INIT_SCALE = 0.1

        def _trunc_normal(key, shape, std):
            return std * jax.random.truncated_normal(key, -2.0, 2.0, shape, dtype=jnp.float32)
        logits = jnp.einsum('bsd,de->bse', x.astype(jnp.float32), router_W) + router_b
        probs = jax.nn.softmax(logits, axis=-1)
        top1 = jnp.argmax(probs, axis=-1)
        mask = jax.nn.one_hot(top1, N_EXPERTS, dtype=x.dtype)
        gates = mask * probs.astype(x.dtype)
        h = jax.nn.relu(jnp.einsum('bsd,edf->besf', x, W1) + b1[:, None, :])
        y = jnp.einsum('besf,efd->besd', h, W2) + b2[:, None, :]
        out = jnp.einsum('bse,besd->bsd', gates, y)
        return out

    def _L1_attn_ref(hidden_states, Wq, Wk, Wv, Wo):
        import jax, jax.numpy as jnp
        import numpy as np
        B, T, HID = (16, 64, 128)
        NH, NKV, D = (8, 4, 128)
        THETA = 10000.0

        def _rotate_half(x):
            x1, x2 = (x[..., :x.shape[-1] // 2], x[..., x.shape[-1] // 2:])
            return jnp.concatenate((-x2, x1), axis=-1)
        b, t, _ = hidden_states.shape
        q = (hidden_states @ Wq).reshape(b, t, NH, D).transpose(0, 2, 1, 3)
        k = (hidden_states @ Wk).reshape(b, t, NKV, D).transpose(0, 2, 1, 3)
        v = (hidden_states @ Wv).reshape(b, t, NKV, D).transpose(0, 2, 1, 3)
        inv_freq = 1.0 / THETA ** (jnp.arange(0, D, 2, dtype=jnp.float32) / D)
        freqs = jnp.outer(jnp.arange(t, dtype=jnp.float32), inv_freq)
        emb = jnp.concatenate((freqs, freqs), axis=-1)
        cos, sin = (jnp.cos(emb), jnp.sin(emb))
        q = q * cos + _rotate_half(q) * sin
        k = k * cos + _rotate_half(k) * sin
        groups = NH // NKV
        k = jnp.repeat(k, groups, axis=1)
        v = jnp.repeat(v, groups, axis=1)
        scale = 1.0 / jnp.sqrt(jnp.float32(D))
        attn = jnp.einsum('bhtd,bhsd->bhts', q, k) * scale
        causal = jnp.triu(jnp.ones((t, t), dtype=bool), k=1)
        attn = jnp.where(causal, -jnp.inf, attn)
        attn = jax.nn.softmax(attn, axis=-1)
        out = jnp.einsum('bhts,bhsd->bhtd', attn, v)
        out = out.transpose(0, 2, 1, 3).reshape(b, t, NH * D)
        return out @ Wo

    def _L1_ffn_ref(x, Wqkv, q_scale, k_scale, Wo, ln_g, ln_b, W1, b1, W2, b2):
        import jax, jax.numpy as jnp
        import numpy as np
        DIM = 128
        DEPTH = 6
        HEADS = 16
        DIM_HEAD = 64
        WINDOW = 32
        INNER = HEADS * DIM_HEAD
        DIM_INNER = int(DIM * 4 * 2 / 3)
        QK_SCALE = 8.0

        def shift_tokens(t):
            a, s = jnp.split(t, 2, -1)
            s = jnp.pad(s, ((0, 0), (1, 0), (0, 0)))[:, :-1]
            return jnp.concatenate([a, s], -1)

        def l2norm(t):
            return t / jnp.maximum(jnp.linalg.norm(t, axis=-1, keepdims=True), 1e-12)

        def rotate_half(x):
            x1, x2 = jnp.split(x, 2, -1)
            return jnp.concatenate([-x2, x1], -1)

        def rotary_tables(n):
            half = jnp.arange(0, DIM_HEAD, 2, dtype=jnp.float32)
            inv_freq = 1.0 / 10000.0 ** (half / DIM_HEAD)
            t = jnp.arange(n, dtype=jnp.float32)
            freqs = t[:, None] * inv_freq[None, :]
            freqs = jnp.concatenate([freqs, freqs], -1)
            base_scale = (half + 0.4 * DIM_HEAD) / (1.4 * DIM_HEAD)
            power = (t - n // 2) / (WINDOW // 2)
            scale = base_scale[None, :] ** power[:, None]
            scale = jnp.concatenate([scale, scale], -1)
            return (freqs, scale)

        def local_attention(q, k, v):
            b, h, n, d = q.shape
            w = WINDOW
            nw = n // w
            bq = q.reshape(b, h, nw, w, d)
            bk = k.reshape(b, h, nw, w, d)
            bv = v.reshape(b, h, nw, w, d)

            def look(t):
                p = jnp.pad(t, ((0, 0), (0, 0), (1, 0), (0, 0), (0, 0)))
                return jnp.concatenate([p[:, :, :nw], p[:, :, 1:]], axis=3)
            bk2, bv2 = (look(bk), look(bv))
            seq = jnp.arange(n).reshape(nw, w)
            seq_p = jnp.pad(seq, ((1, 0), (0, 0)), constant_values=-1)
            jt = jnp.concatenate([seq_p[:nw], seq_p[1:]], axis=1)
            it = seq[:, :, None]
            jb = jt[:, None, :]
            mask = (it < jb) | (it > jb + w) | (jb == -1)
            sim = jnp.einsum('bhwie,bhwje->bhwij', bq, bk2) * QK_SCALE
            sim = jnp.where(mask, -jnp.finfo(sim.dtype).max, sim)
            attn = jax.nn.softmax(sim, -1)
            out = jnp.einsum('bhwij,bhwje->bhwie', attn, bv2)
            return out.reshape(b, h, n, d)

        def attn_layer(x, Wqkv, qs, ksc, Wo):
            b, n, _ = x.shape
            qkv = x @ Wqkv
            q, k, v = jnp.split(qkv, 3, -1)
            sh = lambda t: t.reshape(b, n, HEADS, DIM_HEAD).transpose(0, 2, 1, 3)
            q, k, v = (sh(q), sh(k), sh(v))
            q = l2norm(q) * qs
            k = l2norm(k) * ksc
            freqs, scale = rotary_tables(n)
            cos, sin = (jnp.cos(freqs), jnp.sin(freqs))
            q = q * cos * scale + rotate_half(q) * sin * scale
            inv = 1.0 / scale
            k = k * cos * inv + rotate_half(k) * sin * inv
            out = local_attention(q, k, v)
            out = out.transpose(0, 2, 1, 3).reshape(b, n, INNER)
            return out @ Wo

        def ffn_layer(x, g, bln, W1, b1, W2, b2):
            mu = x.mean(-1, keepdims=True)
            var = ((x - mu) ** 2).mean(-1, keepdims=True)
            xn = (x - mu) / jnp.sqrt(var + 1e-05) * g + bln
            hg = xn @ W1 + b1
            a, gate = jnp.split(hg, 2, -1)
            return a * jax.nn.gelu(gate, approximate=False) @ W2 + b2
        for i in range(DEPTH):
            x = attn_layer(shift_tokens(x), Wqkv[i], q_scale[i], k_scale[i], Wo[i]) + x
            x = ffn_layer(shift_tokens(x), ln_g[i], ln_b[i], W1[i], b1[i], W2[i], b2[i]) + x
        return x
    x = L0_attn_x
    x = _layernorm(x + _L0_attn_ref(x, L0_attn_W_in, L0_attn_conv_w, L0_attn_conv_b, L0_attn_a_param, L0_attn_W_out, L0_attn_ln_w, L0_attn_ln_b), axis=-1)
    x = _layernorm(x + _L0_ffn_ref(x, L0_ffn_router_W, L0_ffn_router_b, L0_ffn_W1, L0_ffn_b1, L0_ffn_W2, L0_ffn_b2), axis=-1)
    x = _layernorm(x + _L1_attn_ref(x, L1_attn_Wq, L1_attn_Wk, L1_attn_Wv, L1_attn_Wo), axis=-1)
    x = _layernorm(x + _L1_ffn_ref(x, L1_ffn_Wqkv, L1_ffn_q_scale, L1_ffn_k_scale, L1_ffn_Wo, L1_ffn_ln_g, L1_ffn_ln_b, L1_ffn_W1, L1_ffn_b1, L1_ffn_W2, L1_ffn_b2), axis=-1)
    return x

_drawn_inputs = setup_inputs


def setup_inputs(seed=0):
    import zlib

    import numpy as np

    out = dict(_drawn_inputs(seed))
    spreads = {'L0_attn_ln_w': (1.0, 0.2),
     'L0_attn_ln_b': (0.0, 0.1),
     'L0_ffn_router_b': (0.0, 0.56),
     'L0_ffn_b1': (0.0, 0.8),
     'L0_ffn_b2': (0.0, 0.543),
     'L1_ffn_q_scale': (1.0, 0.6),
     'L1_ffn_k_scale': (1.0, 0.6),
     'L1_ffn_ln_g': (1.0, 0.6),
     'L1_ffn_ln_b': (0.0, 0.8),
     'L1_ffn_b1': (0.0, 0.8),
     'L1_ffn_b2': (0.0, 0.1)}
    factors = {'L0_ffn_router_W': 4.872,
     'L0_ffn_W1': 8.0,
     'L0_ffn_W2': 8.0,
     'L1_attn_Wq': 8.0,
     'L1_attn_Wk': 8.0,
     'L1_ffn_W1': 3.695,
     'L1_ffn_W2': 3.646}
    for name, (base, spread) in spreads.items():
        noise = np.random.default_rng([zlib.crc32(name.encode()), seed]).standard_normal(out[name].shape)
        drawn = base * np.exp(spread * noise) if base else spread * noise
        out[name] = jnp.asarray(drawn.astype(out[name].dtype))
    for name, factor in factors.items():
        out[name] = (out[name] * factor).astype(out[name].dtype)
    return out
```

```python
from contextlib import ExitStack

import numpy as np

import concourse.bass as bass
from concourse import mybir

F32 = mybir.dt.float32
BF16 = mybir.dt.bfloat16
I32 = mybir.dt.int32
ALU = mybir.AluOpType
ACT = mybir.ActivationFunctionType
AX_X = mybir.AxisListType.X

P = 128
SEQS, TOKENS, D = 4, 512, 128
TILES = TOKENS // P
LN_EPS = 1e-5

TAPS = 5
EXPERTS, FF = 8, 512
FFC = FF // P

HQ, HKV, DH = 8, 4, 128

DEPTH, HEADS, DL = 6, 16, 64
INNER = HEADS * DL
PAIRS = HEADS // 2
WINDOW = 32
PACK = 64
PACKS = P // PACK
KEYS = PACK + WINDOW
QK_SCALE = 8.0
GLU = int(D * 4 * 2 / 3)
GLUC = -(-GLU // P)
GLUP = GLUC * P
GROUP = 4
MASKED = -(2.0 ** 120)

W_QKV, W_O, W_1, W_2 = 0, 3 * INNER, 3 * INNER + PAIRS * D, 3 * INNER + PAIRS * D + 2 * GLUP
W_ALL = W_2 + GLUC * D
C_G, C_B, C_B2, C_B1 = 0, 1, 2, 3
C_ALL = 3 + 2 * GLUC
RSQRT_SEED = float(0x5F3759DF)


class Event:
    def __init__(self, sem, value):
        self.sem, self.value = sem, value


class Lane:

    def __init__(self, name, new_sem):
        self.name, self.new_sem = name, new_sem
        self.steps, self.sems, self.counts, self.waited = [], {}, {}, {}

    def wait(self, *events):
        for ev in events:
            if ev is None or self.waited.get(ev.sem, 0) >= ev.value:
                continue
            self.waited[ev.sem] = ev.value
            self.steps.append(lambda e, ev=ev: e.wait_ge(ev.sem, ev.value))

    def do(self, build, stage=None, by=1):
        if stage is None:
            self.steps.append(build)
            return None
        if stage not in self.sems:
            self.sems[stage] = self.new_sem(f"{self.name}_{stage}")
            self.counts[stage] = 0
        self.counts[stage] += by
        sem = self.sems[stage]
        self.steps.append(lambda e: build(e).then_inc(sem, by))
        return Event(sem, self.counts[stage])

    def play(self, e):
        for step in self.steps:
            step(e)


class Slot:

    def __init__(self, mem):
        self.mem, self.free, self.before, self.ready = mem, [], [], None


class Ring:
    def __init__(self, mems):
        self.slots, self.at = [Slot(m) for m in mems], 0

    def take(self):
        s = self.slots[self.at % len(self.slots)]
        self.at += 1
        assert s.free is not None, "taken again before its readers were queued"
        s.before, s.free = s.free, None
        return s


def build(nc, io):
    ctx = ExitStack()
    with ctx:
        def new_sem(name):
            return ctx.enter_context(nc.semaphore(name))

        def sb(name, shape, dt=F32, stack=None):
            return (stack or ctx).enter_context(nc.sbuf_tensor(name, shape, dt))

        pe, act, dve = Lane("pe", new_sem), Lane("act", new_sem), Lane("dve", new_sem)
        pool, sp = Lane("pool", new_sem), Lane("sp", new_sem)

        def load(dst, src, name):
            return sp.do(lambda e: e.dma_start(dst, src), name, 16)

        def mm(out, lhsT, rhs, start=True, stop=True, stage=None):
            return pe.do(lambda e: e.matmul(out, lhsT, rhs, start=start, stop=stop, skip_group_check=True), stage)

        def turn(out, in_, start=True, stop=True, stage=None):
            ident_ = ident[0:in_.shape[0], 0:in_.shape[0]]
            return pe.do(lambda e: e.matmul(out, in_, ident_, start=start, stop=stop, is_transpose=True,
                                            skip_group_check=True), stage)

        def activate(out, in_, func, stage, **kw):
            return act.do(lambda e: e.activation(out, in_, func, **kw), stage)

        def copy(out, in_, stage):
            return act.do(lambda e: e.activation(out, in_, ACT.Copy), stage)

        def tt(lane, out, a, b, op, stage=None):
            return lane.do(lambda e: e.tensor_tensor(out, a, b, op), stage)

        def ts(out, a, s1, s2, op0, op1=None, stage=None):
            if op1 is None:
                return dve.do(lambda e: e.tensor_scalar(out, a, s1, None, op0), stage)
            return dve.do(lambda e: e.tensor_scalar(out, a, s1, s2, op0, op1), stage)

        def stt(out, a, s, b, op0, op1, stage=None):
            return dve.do(lambda e: e.scalar_tensor_tensor(out=out, in0=a, scalar=s, in1=b, op0=op0, op1=op1), stage)

        def reduce(out, a, op, stage=None, negate=False):
            return dve.do(lambda e: e.tensor_reduce(out, a, AX_X, op, negate=negate), stage)

        def recip(out, a, stage=None):
            return dve.do(lambda e: e.reciprocal(out, a), stage)

        def chained(ev):
            dve.wait(ev)
            return ev

        banks = [ctx.enter_context(nc.psum_tensor(f"bank{i}", [P, 512], F32)) for i in range(8)]
        proj, scores, turned, summed = (Ring(banks[i:i + 2]) for i in (0, 2, 4, 6))

        ident = sb("ident", [P, P])
        identb = sb("identb", [P, P], BF16)
        band = sb("band", [P, 2, GROUP, KEYS], BF16)
        causal = sb("causal", [P, P], BF16)
        xT = sb("xT", [P, SEQS, TOKENS])
        x3T = sb("x3T", [P, SEQS, TOKENS])
        wl = Ring([sb("wl0", [P, W_ALL])])
        cl = [sb(f"cl{i}", [P, C_ALL]) for i in range(2)]
        stats = sb("stats", [P, TILES, 6])
        moments = sb("moments", [P, TILES, 2])
        rstd = sb("rstd", [P, TILES])
        nw = sb("nw", [P, 3, 32])

        c_ev = load(ident[:, :], io["ident"], "const")
        pe.wait(c_ev)

        def inverse_root(out, src, guard, op):
            n = src.shape[-1] if len(src.shape) == 2 else src.shape[1]
            x, y, t = (nw[:, i, 0:n] for i in range(3))
            chained(ts(x, src, guard, None, op, stage="newton"))
            chained(ts(t.bitcast(I32), x.bitcast(I32), 1, None, ALU.arith_shift_right, stage="newton"))
            chained(ts(y.bitcast(I32), t.bitcast(I32), -1.0, RSQRT_SEED, ALU.mult, ALU.add, stage="newton"))
            for k in range(3):
                chained(stt(t, y, -0.5, y, ALU.mult, ALU.mult, stage="newton"))
                chained(tt(dve, t, t, x, ALU.mult, stage="newton"))
                to = y if k < 2 else out
                ev = chained(stt(to, t, 1.5, y, ALU.add, ALU.mult, stage="newton"))
            return ev

        def layer_norm(dst, src, stage):
            for t in range(TILES):
                ev = dve.do(lambda e, t=t: e.bn_stats(stats[:, t, :], src[:, t, :]), "bn_stats")
            chained(ev)
            for t in range(TILES):
                ev = dve.do(lambda e, t=t: e.bn_aggr(moments[:, t, :], stats[:, t, :]), "bn_aggr")
            chained(ev)
            inverse_root(rstd[:, :], moments[:, :, 1], LN_EPS, ALU.add)
            for t in range(TILES):
                ev = ts(dst[:, t, :], src[:, t, :], moments[:, t, 0:1], rstd[:, t:t + 1],
                        ALU.subtract, ALU.mult, stage=stage)
            return ev

        def turn_tiles(src, events, stage):
            s = turned.take()
            pe.wait(*s.before, *events)
            for t in range(TILES):
                ev = turn(s.mem[:, t * P:(t + 1) * P], src(t), stage=stage if t == TILES - 1 else None)
            s.ready = ev
            return s

        def load_layer(l):
            w = wl.take()
            sp.wait(*w.before)
            w.ready = load(w.mem[:, :], io["wl"][l], f"weights{l % 2}")
            w.ready2 = load(cl[l % 2][:, :], io["cl"][l], f"columns{l % 2}")
            return w

        early = ExitStack()
        with early:
            def eb(name, shape, dt=F32):
                return sb(name, shape, dt, early)

            x0T = xT
            x0 = Ring([eb(f"x0_{i}", [P, TILES, D]) for i in range(2)])
            w_in = eb("w_in", [P, 2 * D])
            w_out = eb("w_out", [P, D])
            ccols = eb("ccols", [P, TAPS + 2])
            lnrow = eb("lnrow", [P, 2, D])
            rw = eb("rw", [P, EXPERTS])
            rrow = eb("rrow", [P, 2, EXPERTS])
            w1 = eb("w1", [P, EXPERTS, FF])
            w2 = eb("w2", [P, EXPERTS, FFC, D])
            b1 = eb("b1", [P, EXPERTS, FFC])
            b2 = eb("b2", [EXPERTS, D])
            wqkv = eb("wqkv", [P, (HQ + 2 * HKV) * DH])
            wo = eb("wo", [P, HQ, D])
            rope = eb("rope", [P, 2, TILES, DH])

            band32 = eb("band32", [P, 2, GROUP, KEYS])
            causal32 = eb("causal32", [P, P])
            load(band32[:, :, :, :], io["band"], "masks")
            masks_ev = load(causal32[:, :], io["causal"], "masks")
            act.wait(c_ev, masks_ev)
            copy(identb[:, :], ident[:, :], "masks")
            copy(band[:, :, :, :], band32[:, :, :, :], "masks")
            pe.wait(copy(causal[:, :], causal32[:, :], "masks"))

            io_ev = {}
            for dst, name in ((x0T, "x0T"), (w_in, "w_in"), (ccols, "ccols"), (w_out, "w_out"),
                              (lnrow, "lnrow"), (rw, "rw"), (rrow, "rrow"), (w1, "w1"), (b1, "b1"), (b2, "b2"),
                              (w2, "w2"), (wqkv, "wqkv"), (rope, "rope"), (wo, "wo")):
                full = dst[tuple(slice(None) for _ in dst.shape)]
                io_ev[name] = load(full, io[name], "load_" + name)

            gate = eb("gate", [P, TOKENS])
            val = eb("val", [P, TOKENS + TAPS - 1])
            conv = eb("conv", [P, TOKENS])
            y = eb("y", [P, TOKENS])
            resT = eb("resT", [P, TOKENS])
            tokA = eb("tokA", [P, TILES, D])
            x1 = eb("x1", [P, TILES, D])
            x1T = eb("x1T", [P, TOKENS])
            decay = eb("decay", [P, 1])

            edge_ev = dve.do(lambda e: e.memset(val[:, :], 0.0), "edges")
            act.wait(io_ev["ccols"])
            decay_ev = activate(decay[:, :], ccols[:, TAPS + 1:TAPS + 2], ACT.Tanh, "decay")
            act.wait(edge_ev)
            dve.wait(decay_ev)

            free = {k: [] for k in ("gate", "val", "y", "resT", "x1T", "x1", "x2T", "h")}
            x1_ev, x1T_ev = None, None

            def load_x0(b):
                s = x0.take()
                sp.wait(*s.before)
                s.ready = load(s.mem[:, :, :], io["x0"][b], f"x0_{b % 2}")
                return s

            x0_tok = {0: load_x0(0), 1: load_x0(1)}

            def gated_scan(b):
                sg = proj.take()
                pe.wait(*sg.before, io_ev["x0T"], io_ev["w_in"])
                g_ev = mm(sg.mem[:, :], w_in[:, 0:D], x0T[:, b, :], stage="gate")
                sv = proj.take()
                pe.wait(*sv.before)
                v_ev = mm(sv.mem[:, :], w_in[:, D:2 * D], x0T[:, b, :], stage="val")
                act.wait(g_ev, *free["gate"])
                sig_ev = activate(gate[:, :], sg.mem[:, :], ACT.Sigmoid, "sigmoid")
                sg.free = [sig_ev]
                act.wait(v_ev, *free["val"])
                val_ev = copy(val[:, TAPS // 2:TAPS // 2 + TOKENS], sv.mem[:, :], "val")
                sv.free = [val_ev]
                dve.wait(val_ev, io_ev["ccols"])
                chained(ts(conv[:, :], val[:, 0:TOKENS], ccols[:, 0:1], ccols[:, TAPS:TAPS + 1],
                           ALU.mult, ALU.add, stage="conv"))
                for k in range(1, TAPS):
                    ev = chained(stt(conv[:, :], val[:, k:k + TOKENS], ccols[:, k:k + 1], conv[:, :],
                                     ALU.mult, ALU.add, stage="conv"))
                free["val"] = [ev]
                dve.wait(sig_ev)
                ev = chained(tt(dve, conv[:, :], conv[:, :], gate[:, :], ALU.mult, stage="conv"))
                free["gate"] = [ev]
                dve.wait(*free["y"])
                scan_ev = dve.do(lambda e: e.tensor_tensor_scan(
                    y[:, :], decay[:, 0:1].to_broadcast([P, TOKENS]), conv[:, :], 0.0, ALU.mult, ALU.add), "scan")
                so = proj.take()
                pe.wait(*so.before, scan_ev, io_ev["w_out"])
                o_ev = mm(so.mem[:, :], w_out[:, :], y[:, :], stage="w_out")
                free["y"] = [o_ev]
                dve.wait(o_ev, *free["resT"], scan_ev)
                res_ev = tt(dve, resT[:, :], so.mem[:, :], x0T[:, b, :], ALU.add, stage="res")
                so.free = [res_ev]
                s = turn_tiles(lambda t: resT[:, t * P:(t + 1) * P], [res_ev], "res_tok")
                free["resT"] = [s.ready]
                dve.wait(s.ready)
                ln_ev = layer_norm(tokA, s.mem[:, :].rearrange("p (t d) -> p t d", t=TILES), "ln0")
                s.free = [ln_ev]
                dve.wait(ln_ev, io_ev["lnrow"], x0_tok[b].ready)
                chained(tt(dve, tokA[:, :, :], tokA[:, :, :], lnrow[:, 0:1, :].to_broadcast([P, TILES, D]),
                           ALU.mult, stage="affine"))
                chained(tt(dve, tokA[:, :, :], tokA[:, :, :], lnrow[:, 1:2, :].to_broadcast([P, TILES, D]),
                           ALU.add, stage="affine"))
                ev = chained(tt(dve, tokA[:, :, :], tokA[:, :, :], x0_tok[b].mem[:, :, :], ALU.add, stage="affine"))
                x0_tok[b].free = [ev]
                if b + 2 < SEQS:
                    x0_tok[b + 2] = load_x0(b + 2)
                dve.wait(*free["x1"])
                x1_ev = layer_norm(x1, tokA, "x1")
                s = turn_tiles(lambda t: x1[:, t, :], [x1_ev], "x1T")
                act.wait(s.ready, *free["x1T"])
                x1T_ev = copy(x1T[:, :], s.mem[:, :], "x1T")
                s.free = [x1T_ev]
                return x1_ev, x1T_ev

            lg = eb("lg", [P, TILES, EXPERTS])
            pr = eb("pr", [P, TILES, EXPERTS])
            rowst = eb("rowst", [P, 4, TILES])
            gates = eb("gates", [P, TILES, EXPERTS])
            gatesT = eb("gatesT", [EXPERTS, TOKENS])
            hbuf = Ring([eb(f"hbuf{i}", [P, FFC, TOKENS]) for i in range(2)])
            acc = eb("acc", [P, TILES, D])
            x2T = eb("x2T", [P, TOKENS])

            def per_tile(col):
                return col.unsqueeze(2).to_broadcast([P, TILES, EXPERTS])

            def router(x1T_ev, x1_ev):
                s = proj.take()
                pe.wait(*s.before, x1T_ev, io_ev["rw"])
                for t in range(TILES):
                    ev = mm(s.mem[:, t * EXPERTS:(t + 1) * EXPERTS], x1T[:, t * P:(t + 1) * P], rw[:, :],
                            stage="logits" if t == TILES - 1 else None)
                dve.wait(ev, io_ev["rrow"])
                ev = chained(tt(dve, lg[:, :, :], s.mem[:, 0:TILES * EXPERTS].rearrange("p (t e) -> p t e", t=TILES),
                                rrow[:, 0:1, :].to_broadcast([P, TILES, EXPERTS]), ALU.add, stage="router"))
                s.free = [ev]
                chained(reduce(rowst[:, 0, :], lg[:, :, :], ALU.max, stage="router"))
                ev = chained(tt(dve, lg[:, :, :], lg[:, :, :], per_tile(rowst[:, 0, :]), ALU.subtract, stage="router"))
                act.wait(ev)
                ev = activate(pr[:, :, :], lg[:, :, :], ACT.Exp, "router_exp")
                dve.wait(ev)
                chained(reduce(rowst[:, 1, :], pr[:, :, :], ALU.add, stage="router"))
                chained(recip(rowst[:, 2, :], rowst[:, 1, :], stage="router"))
                chained(tt(dve, pr[:, :, :], pr[:, :, :], per_tile(rowst[:, 2, :]), ALU.mult, stage="router"))
                chained(reduce(rowst[:, 0, :], pr[:, :, :], ALU.max, stage="router"))
                chained(tt(dve, lg[:, :, :], pr[:, :, :], per_tile(rowst[:, 0, :]), ALU.is_equal, stage="router"))
                chained(tt(dve, lg[:, :, :], lg[:, :, :], rrow[:, 1:2, :].to_broadcast([P, TILES, EXPERTS]),
                           ALU.mult, stage="router"))
                chained(reduce(rowst[:, 3, :], lg[:, :, :], ALU.max, stage="router"))
                chained(tt(dve, lg[:, :, :], lg[:, :, :], per_tile(rowst[:, 3, :]), ALU.is_equal, stage="router"))
                g_ev = chained(tt(dve, gates[:, :, :], lg[:, :, :], pr[:, :, :], ALU.mult, stage="router"))
                s = turned.take()
                pe.wait(*s.before, g_ev)
                for t in range(TILES):
                    ev = turn(s.mem[0:EXPERTS, t * P:(t + 1) * P], gates[:, t, :],
                              stage="gatesT" if t == TILES - 1 else None)
                act.wait(ev)
                gT_ev = copy(gatesT[:, :], s.mem[0:EXPERTS, :], "gatesT")
                s.free = [gT_ev]
                s = proj.take()
                pe.wait(*s.before, gT_ev, io_ev["b2"])
                for t in range(TILES):
                    ev = mm(s.mem[:, t * D:(t + 1) * D], gatesT[:, t * P:(t + 1) * P], b2[:, :],
                            stage="gate_b2" if t == TILES - 1 else None)
                dve.wait(ev, x1_ev)
                ev = chained(tt(dve, acc[:, :, :], s.mem[:, :].rearrange("p (t d) -> p t d", t=TILES), x1[:, :, :],
                                ALU.add, stage="acc"))
                s.free = [ev]
                return ev

            def experts(x1T_ev):
                def up(e_):
                    h = hbuf.take()
                    for c in range(FFC):
                        s = proj.take()
                        pe.wait(*s.before, x1T_ev, io_ev["w1"])
                        ev = mm(s.mem[:, :], w1[:, e_, c * P:(c + 1) * P], x1T[:, :], stage="up")
                        act.wait(ev, *h.before, io_ev["b1"])
                        s.free = [activate(h.mem[:, c, :], s.mem[:, :], ACT.Relu, "relu", bias=b1[:, e_, c:c + 1])]
                        h.ready = s.free[0]
                    return h

                def down(e_, h):
                    s = summed.take()
                    pe.wait(*s.before, h.ready, io_ev["w2"])
                    for t in range(TILES):
                        for c in range(FFC):
                            ev = mm(s.mem[:, t * D:(t + 1) * D], h.mem[:, c, t * P:(t + 1) * P], w2[:, e_, c, :],
                                    start=c == 0, stop=c == FFC - 1,
                                    stage="down" if (t, c) == (TILES - 1, FFC - 1) else None)
                    h.free = [ev]
                    dve.wait(ev)
                    for t in range(TILES):
                        ev = stt(acc[:, t, :], s.mem[:, t * D:(t + 1) * D], gates[:, t, e_:e_ + 1], acc[:, t, :],
                                 ALU.mult, ALU.add, stage="acc")
                    s.free = [ev]
                    dve.wait(ev)
                    return ev

                last = up(0)
                for e_ in range(1, EXPERTS):
                    nxt = up(e_)
                    down(e_ - 1, last)
                    last = nxt
                return down(EXPERTS - 1, last)

            prod = Ring([eb(f"prod{i}", [P, 2, GROUP, DH]) for i in range(2)])
            q2T = eb("q2T", [P, HQ, TOKENS])
            k2T = eb("k2T", [P, HKV, TOKENS])
            v2 = eb("v2", [P, TILES, HKV * DH])
            prob2 = Ring([eb(f"prob2{i}", [P, TOKENS]) for i in range(3)])
            prob2T = Ring([eb(f"prob2T{i}", [P, TILES, P]) for i in range(2)])
            soft2 = Ring([eb(f"soft2{i}", [P, 4]) for i in range(4)])
            o2 = eb("o2", [P, HQ, DH])
            o2T = Ring([eb(f"o2T{i}", [P, HQ, P]) for i in range(2)])
            free.update({"q2T": [], "k2T": [], "v2": [], "o2": []})
            scale2 = 1.0 / float(np.sqrt(np.float32(DH)))

            def qkv2(x2T_ev):
                half = DH // 2
                for t in range(TILES):
                    for c in range(4):
                        s = proj.take()
                        pe.wait(*s.before, x2T_ev, io_ev["wqkv"])
                        ev = mm(s.mem[:, :], x2T[:, t * P:(t + 1) * P], wqkv[:, c * 512:(c + 1) * 512], stage="qkv2")
                        if c == 3:
                            act.wait(ev, *free["v2"])
                            v_ev = copy(v2[:, t, :], s.mem[:, :], "v2")
                            s.free = [v_ev]
                            continue
                        w = prod.take()
                        dve.wait(ev, *w.before, io_ev["rope"])
                        src = s.mem[:, :].rearrange("p (h d) -> p h d", h=GROUP)

                        def table(k, lo, hi):
                            return rope[:, k, t, lo:hi].unsqueeze(1).to_broadcast([P, GROUP, hi - lo])
                        tt(dve, w.mem[:, 0, :, :], src, table(0, 0, DH), ALU.mult)
                        tt(dve, w.mem[:, 1, :, 0:half], src[:, :, half:DH], table(1, 0, half), ALU.mult)
                        r_ev = tt(dve, w.mem[:, 1, :, half:DH], src[:, :, 0:half], table(1, half, DH), ALU.mult,
                                  stage="rope2")
                        s.free = [r_ev]
                        z = turned.take()
                        pe.wait(*z.before, r_ev)
                        for j in range(GROUP):
                            turn(z.mem[:, j * P:(j + 1) * P], w.mem[:, 0, j, :], stop=False)
                            ev = turn(z.mem[:, j * P:(j + 1) * P], w.mem[:, 1, j, :], start=False,
                                      stage="rope2T" if j == GROUP - 1 else None)
                        w.free = [ev]
                        dst = (q2T[:, c * GROUP:(c + 1) * GROUP, t * P:(t + 1) * P] if c < 2
                               else k2T[:, :, t * P:(t + 1) * P])
                        act.wait(ev, *free["q2T"], *free["k2T"])
                        qk_ev = copy(dst, z.mem[:, :].rearrange("p (j t) -> p j t", j=GROUP), "qk2T")
                        z.free = [qk_ev]
                return qk_ev, v_ev

            def attend2(qk_ev, v_ev, x2T_ev):
                work = [(t, h) for t in range(TILES) for h in range(HQ)]
                kept = {}

                def score(t, h):
                    n = (t + 1) * P
                    s = scores.take()
                    pe.wait(*s.before, qk_ev)
                    mm(s.mem[:, 0:n], q2T[:, h, t * P:(t + 1) * P], k2T[:, h // 2, 0:n], stop=False)
                    ev = mm(s.mem[:, n - P:n], identb[:, :], causal[:, :], start=False, stage="score2")
                    m, p = soft2.take(), prob2.take()
                    dve.wait(ev, *m.before)
                    chained(reduce(m.mem[:, 0:1], s.mem[:, 0:n], ALU.max, stage="max2"))
                    b_ev = ts(m.mem[:, 1:2], m.mem[:, 0:1], -scale2, None, ALU.mult, stage="max2")
                    act.wait(b_ev, *p.before)
                    e_ev = activate(p.mem[:, 0:n], s.mem[:, 0:n], ACT.Exp, "exp2", scale=scale2,
                                    bias=m.mem[:, 1:2], accum_out=m.mem[:, 2:3])
                    s.free = [e_ev]
                    kept[t, h] = (m, p, e_ev)

                def weigh(t, h):
                    m, p, e_ev = kept.pop((t, h))
                    z = turned.take()
                    pe.wait(*z.before, e_ev)
                    for k in range(t + 1):
                        ev = turn(z.mem[:, k * P:(k + 1) * P], p.mem[:, k * P:(k + 1) * P],
                                  stage="prob2T" if k == t else None)
                    p.free = [ev]
                    q = prob2T.take()
                    act.wait(ev, *q.before)
                    c_ev = copy(q.mem[:, 0:t + 1, :], z.mem[:, 0:(t + 1) * P].rearrange("p (k q) -> p k q", q=P),
                                "prob2T")
                    z.free = [c_ev]
                    o = summed.take()
                    pe.wait(*o.before, c_ev, v_ev)
                    for k in range(t + 1):
                        ev = mm(o.mem[:, 0:DH], q.mem[:, k, :], v2[:, k, (h // 2) * DH:(h // 2 + 1) * DH],
                                start=k == 0, stop=k == t, stage="pv2" if k == t else None)
                    q.free = [ev]
                    if h == 0:
                        dve.wait(*free["o2"])
                    dve.wait(e_ev)
                    chained(recip(m.mem[:, 3:4], m.mem[:, 2:3], stage="norm2"))
                    dve.wait(ev)
                    n_ev = ts(o2[:, h, :], o.mem[:, 0:DH], m.mem[:, 3:4], None, ALU.mult, stage="norm2")
                    o.free = [n_ev]
                    m.free = [n_ev]
                    if h == HQ - 1:
                        d = o2T.take()
                        for g in range(HQ // GROUP):
                            z = turned.take()
                            pe.wait(*z.before, n_ev)
                            for j in range(GROUP):
                                ev = turn(z.mem[:, j * P:(j + 1) * P], o2[:, g * GROUP + j, :],
                                          stage="o2T" if j == GROUP - 1 else None)
                            act.wait(ev, *d.before)
                            z.free = [copy(d.mem[:, g * GROUP:(g + 1) * GROUP, :],
                                           z.mem[:, :].rearrange("p (j t) -> p j t", j=GROUP), "o2T")]
                            d.ready = z.free[0]
                        free["o2"] = [ev]
                        s = proj.take()
                        pe.wait(*s.before, d.ready, io_ev["wo"])
                        for k in range(HQ):
                            ev = mm(s.mem[:, 0:P], wo[:, k, :], d.mem[:, k, :], start=k == 0, stop=k == HQ - 1,
                                    stage="wo2" if k == HQ - 1 else None)
                        d.free = [ev]
                        dve.wait(ev, x2T_ev, *free["resT"])
                        r_ev = tt(dve, resT[:, t * P:(t + 1) * P], s.mem[:, 0:P], x2T[:, t * P:(t + 1) * P],
                                  ALU.add, stage="res")
                        s.free = [r_ev]
                        return r_ev
                    return None

                for i in range(len(work) + 1):
                    if i < len(work):
                        score(*work[i])
                    if i:
                        ev = weigh(*work[i - 1])
                free["q2T"] = free["k2T"] = free["v2"] = [Event(pe.sems["pv2"], pe.counts["pv2"])]
                return ev

            def sequence(b):
                x1_ev, x1T_ev = gated_scan(b)
                router(x1T_ev, x1_ev)
                acc_ev = experts(x1T_ev)
                free["x1"] = [acc_ev]
                free["x1T"] = [Event(pe.sems["up"], pe.counts["up"])]
                dve.wait(acc_ev)
                ln_ev = layer_norm(tokA, acc, "x2")
                s = turn_tiles(lambda t: tokA[:, t, :], [ln_ev], "x2T")
                dve.wait(s.ready)
                act.wait(s.ready, *free["x2T"])
                x2T_ev = copy(x2T[:, :], s.mem[:, :], "x2T")
                s.free = [x2T_ev]
                qk_ev, v_ev = qkv2(x2T_ev)
                r_ev = attend2(qk_ev, v_ev, x2T_ev)
                free["x2T"] = [r_ev]
                s = turn_tiles(lambda t: resT[:, t * P:(t + 1) * P], [r_ev], "res2_tok")
                free["resT"] = [s.ready]
                dve.wait(s.ready)
                ln_ev = layer_norm(tokA, s.mem[:, :].rearrange("p (t d) -> p t d", t=TILES), "x3")
                s.free = [ln_ev]
                s = turn_tiles(lambda t: tokA[:, t, :], [ln_ev], "x3T")
                dve.wait(s.ready)
                act.wait(s.ready)
                copy(xT[:, b, :], s.mem[:, :], "x3T")
                ev = copy(x3T[:, b, :], s.mem[:, :], "x3T")
                s.free = [ev]
                return ev

            layer_w = {0: load_layer(0)}
            x3_ev = [sequence(b) for b in range(SEQS)]

        ends = []
        for src in (pe, act, dve):
            ends += [Event(src.sems[k], src.counts[k]) for k in src.sems]
        for lane in (pe, act, dve, pool, sp):
            lane.wait(*ends)

        wl.slots.append(Slot(sb("wl1", [P, W_ALL])))
        wl.at = 1
        base = sb("base", [P, 4, TILES, DL])
        table = sb("table", [P, 4, TILES, DL])
        qkrow = [sb(f"qkrow{i}", [P, 4, DL]) for i in range(2)]
        base_ev = load(base[:, :, :, :], io["base"], "base")

        xs = Ring([sb(f"xs{i}", [P, WINDOW + TOKENS]) for i in range(2)])
        xf = Ring([sb("xf0", [P, TOKENS])])
        raw = Ring([sb(f"raw{i}", [P, 2 * HEADS, DL]) for i in range(3)])
        sq = Ring([sb(f"sq{i}", [P, 8, DL]) for i in range(2)])
        rot = Ring([sb(f"rot{i}", [P, 2 * HEADS, DL]) for i in range(1)])
        n2 = Ring([sb(f"n2{i}", [P, 2 * HEADS]) for i in range(2)])
        rn = Ring([sb(f"rn{i}", [P, 2 * HEADS]) for i in range(2)])
        qT = Ring([sb(f"qT{i}", [P, PAIRS, P]) for i in range(2)])
        kT = Ring([sb(f"kT{i}", [P, PAIRS, WINDOW + P]) for i in range(3)])
        vp = Ring([sb(f"vp{i}", [KEYS, PACKS, HEADS, DL + 1]) for i in range(3)])
        soft = Ring([sb(f"soft{i}", [P, 2, GROUP]) for i in range(4)])
        prob = Ring([sb(f"prob{i}", [P, GROUP, KEYS]) for i in range(3)])
        probT = Ring([sb(f"probT{i}", [KEYS, GROUP, P]) for i in range(2)])
        ot = Ring([sb(f"ot{i}", [P, HEADS, DL]) for i in range(2)])
        oT = Ring([sb("oT0", [P, PAIRS, TOKENS])])
        xn = sb("xn", [P, TILES, D])
        xnT = sb("xnT", [P, TOKENS])
        glu = Ring([sb(f"glu{i}", [P, TOKENS]) for i in range(2)])
        hT = Ring([sb("hT0", [P, GLUC, TOKENS])])

        TOTAL = DEPTH * SEQS * TILES
        GROUPS = HEADS // GROUP
        x_ev = list(x3_ev)
        xs_of, tab_ev, tab_free = {}, {}, {0: [], 1: [], "last": []}
        state = {}
        batch = {}
        out_ev = []

        def where(n):
            return n // (SEQS * TILES), n // TILES % SEQS, n % TILES

        last_pool = [None]

        def on_pool(build_, stage):
            pool.wait(last_pool[0])
            last_pool[0] = pool.do(build_, stage)
            return last_pool[0]

        def unit(x, inverse):
            return on_pool(lambda e: e.tensor_tensor(x, x, inverse, ALU.mult), "unit")

        def shifted(dst, b, stage):
            on_pool(lambda e: e.memset(dst[D // 2:D, 0:1], 0.0), stage)
            on_pool(lambda e: e.tensor_copy(dst[0:D // 2, :], xT[0:D // 2, b, :]), stage)
            return on_pool(lambda e: e.tensor_copy(dst[D // 2:D, 1:TOKENS], xT[D // 2:D, b, 0:TOKENS - 1]), stage)

        for s in xs.slots:
            ones_ev = on_pool(lambda e, s=s: e.memset(s.mem[:, 0:WINDOW + 1], 0.0), "fill")
        for s in vp.slots:
            ones_ev = on_pool(lambda e, s=s: e.memset(s.mem[:, :, :, DL:DL + 1], 1.0), "fill")
        pe.wait(ones_ev)
        act.wait(ones_ev)
        pool.wait(ones_ev)

        def tables(l):
            row = qkrow[l % 2]
            sp.wait(*tab_free[l % 2])
            r_ev = load(row[:, :, :], io["qkrow"][l], f"qkrow{l % 2}")
            dve.wait(r_ev, base_ev, *tab_free["last"])
            for k in range(4):
                ev = tt(dve, table[:, k, :, :], base[:, k, :, :],
                        row[:, k:k + 1, :].to_broadcast([P, TILES, DL]), ALU.mult, stage="tables")
            tab_ev[l] = ev

        def project(n, part):
            l, b, t = where(n)
            if part == 0:
                if t == 0:
                    s = xs.take()
                    pool.wait(*s.before, x_ev[b])
                    s.ready = shifted(s.mem[:, WINDOW:WINDOW + TOKENS], b, "xs")
                    xs_of[l, b] = s
                state[n] = {"raw": raw.take(), "n2": n2.take(), "rn": rn.take()}
            st, s, w = state[n], xs_of[l, b], layer_w[l]
            bank = proj.take()
            pe.wait(*bank.before, s.ready, w.ready)
            ev = mm(bank.mem[:, :], s.mem[:, WINDOW + t * P:WINDOW + (t + 1) * P],
                    w.mem[:, part * 512:(part + 1) * 512], stage="qk")
            q = sq.take()
            act.wait(ev, *q.before, *st["raw"].before)
            q_ev = activate(q.mem[:, :, :], bank.mem[:, :].rearrange("p (h d) -> p h d", d=DL), ACT.Square, "square")
            raw_ev = copy(st["raw"].mem[:, part * 8:(part + 1) * 8, :],
                          bank.mem[:, :].rearrange("p (h d) -> p h d", d=DL), "raw")
            bank.free = [raw_ev]
            dve.wait(q_ev, *st["n2"].before)
            n_ev = reduce(st["n2"].mem[:, part * 8:(part + 1) * 8], q.mem[:, :, :], ALU.add, stage="norm2sum")
            q.free = [n_ev]
            if part == 3:
                dve.wait(n_ev, *st["rn"].before)
                r_ev = inverse_root(st["rn"].mem[:, :], st["n2"].mem[:, :], 1e-24, ALU.max)
                st["n2"].free = [r_ev]
                pool.wait(r_ev, raw_ev)
                r = st["raw"]
                for h in (0, 1):
                    hs = slice(h * HEADS, (h + 1) * HEADS)
                    r.ready = unit(r.mem[:, hs, :], st["rn"].mem[:, hs].unsqueeze(2).to_broadcast([P, HEADS, DL]))
                st["rn"].free = [r.ready]

        def project_v(n, part):
            l, b, t = where(n)
            st, s, w = state[n], xs_of[l, b], layer_w[l]
            if part == 0:
                st["vp"] = vp.take()
            a, half = part // 2, part % 2
            bank = proj.take()
            pe.wait(*bank.before, s.ready, w.ready)
            ev = mm(bank.mem[0:KEYS, :], s.mem[:, t * P + a * PACK:t * P + a * PACK + KEYS],
                    w.mem[:, 2 * INNER + half * 512:2 * INNER + (half + 1) * 512], stage="v")
            act.wait(ev, *st["vp"].before)
            v_ev = copy(st["vp"].mem[:, a, half * 8:(half + 1) * 8, 0:DL],
                        bank.mem[0:KEYS, :].rearrange("p (h d) -> p h d", d=DL), "v")
            bank.free = [v_ev]
            if part == 3:
                st["vp"].ready = v_ev
                if t == TILES - 1:
                    s.free = [ev]

        def rotate(n, part):
            l, b, t = where(n)
            st = state[n]
            if part == 0:
                if n % (SEQS * TILES) == 0:
                    tables(l)
                    if l == 0:
                        layer_w[1] = load_layer(1)
                st["rot"], st["qT"], st["kT"] = rot.take(), qT.take(), kT.take()
                k = st["kT"]
                if t == 0:
                    pool.wait(*k.before)
                    k.edge = on_pool(lambda e: e.memset(k.mem[:, :, 0:WINDOW], 0.0), "kT_edge")
            r, v = st["raw"], st["rot"]
            hs = slice(part * 8, (part + 1) * 8)
            which = 0 if part < 2 else 2
            half = DL // 2

            def tab(k, lo, hi):
                return table[:, k, t, lo:hi].unsqueeze(1).to_broadcast([P, 8, hi - lo])
            dve.wait(r.ready, tab_ev[l], *v.before)
            tt(dve, v.mem[:, hs, 0:half], r.mem[:, hs, half:DL], tab(which + 1, 0, half), ALU.mult)
            ev = tt(dve, v.mem[:, hs, half:DL], r.mem[:, hs, 0:half], tab(which + 1, half, DL), ALU.mult,
                    stage="rot_sin")
            dve.wait(ev)
            ev = tt(dve, r.mem[:, hs, :], r.mem[:, hs, :], tab(which, 0, DL), ALU.mult, stage="rot_cos")
            if n % (SEQS * TILES) == SEQS * TILES - 1:
                tab_free.update({l % 2: [ev], "last": [ev]})
            z = turned.take()
            pe.wait(*z.before, ev)
            for j in range(4):
                two = slice(part * 8 + 2 * j, part * 8 + 2 * j + 2)
                turn(z.mem[:, j * P:(j + 1) * P], r.mem[:, two, :], stop=False)
                ev = turn(z.mem[:, j * P:(j + 1) * P], v.mem[:, two, :], start=False,
                          stage="qkT" if j == 3 else None)
            ps = slice((part % 2) * 4, (part % 2) * 4 + 4)
            if part < 2:
                q = st["qT"]
                act.wait(ev, *q.before)
                c_ev = copy(q.mem[:, ps, :], z.mem[:, :].rearrange("p (j t) -> p j t", j=4), "qT")
                q.ready = c_ev
            else:
                k = st["kT"]
                act.wait(ev, *k.before)
                c_ev = copy(k.mem[:, ps, WINDOW:WINDOW + P], z.mem[:, :].rearrange("p (j t) -> p j t", j=4), "kT")
                k.ready = c_ev
            z.free = [c_ev]
            if part == 3:
                r.free, v.free = [ev], [ev]
                if t < TILES - 1:
                    nxt = kT.slots[kT.at % len(kT.slots)]
                    k = st["kT"]
                    pool.wait(k.ready, *nxt.free)
                    nxt.edge = on_pool(lambda e: e.tensor_copy(nxt.mem[:, :, 0:WINDOW], k.mem[:, :, P:P + WINDOW]),
                                       "kT_edge")
                    st["edge_copied"] = nxt.edge

        def score(n, g):
            l, b, t = where(n)
            st = state[n]
            q, k = st["qT"], st["kT"]
            parity, first = g % 2, 4 * (g // 2)
            s = scores.take()
            pe.wait(*s.before, q.ready, k.ready, k.edge)
            mm(s.mem[:, 0:GROUP * KEYS], identb[:, :], band[:, 1 if t == 0 else 0, :, :], stop=False)
            rows = slice(parity * DL, (parity + 1) * DL)
            for j in range(GROUP):
                for a in range(PACKS):
                    ev = mm(s.mem[a * PACK:(a + 1) * PACK, j * KEYS:(j + 1) * KEYS],
                            q.mem[rows, first + j, a * PACK:(a + 1) * PACK],
                            k.mem[rows, first + j, a * PACK:a * PACK + KEYS], start=False,
                            stage="score" if (j, a) == (GROUP - 1, PACKS - 1) else None)
            if g == GROUPS - 1:
                q.free, k.free = [ev], [ev, st.get("edge_copied")]
            m, p = soft.take(), prob.take()
            view = s.mem[:, 0:GROUP * KEYS].rearrange("p (j k) -> p j k", j=GROUP)
            dve.wait(ev, *m.before, *p.before)
            dve.wait(reduce(m.mem[:, 0, :], view, ALU.max, stage="max"))
            d_ev = tt(dve, p.mem[:, :, :], view, m.mem[:, 0, :].unsqueeze(2).to_broadcast([P, GROUP, KEYS]),
                      ALU.subtract, stage="less_max")
            s.free = [d_ev]
            act.wait(d_ev)
            p.ready = activate(p.mem[:, :, :], p.mem[:, :, :], ACT.Exp, "exp", scale=QK_SCALE)
            st[g] = (m, p)

        def turn_prob(n, g):
            st = state[n]
            m, p = st[g]
            z, pt = turned.take(), probT.take()
            pe.wait(*z.before, p.ready)
            for j in range(GROUP):
                ev = turn(z.mem[0:KEYS, j * P:(j + 1) * P], p.mem[:, j, :], stage="probT" if j == GROUP - 1 else None)
            p.free = [ev]
            act.wait(ev, *pt.before)
            pt.ready = copy(pt.mem[:, :, :], z.mem[0:KEYS, :].rearrange("p (j q) -> p j q", j=GROUP), "probT")
            z.free = [pt.ready]
            st[g] = (m, pt)

        def weigh(n, g):
            st = state[n]
            m, pt = st[g]
            v = st["vp"]
            parity, first = g % 2, 4 * (g // 2)
            s = summed.take()
            pe.wait(*s.before, pt.ready, v.ready)
            for j in range(GROUP):
                head = 2 * (first + j) + parity
                for a in range(PACKS):
                    ev = mm(s.mem[a * PACK:(a + 1) * PACK, j * (DL + 1):(j + 1) * (DL + 1)],
                            pt.mem[:, j, a * PACK:(a + 1) * PACK], v.mem[:, a, head, :],
                            stage="weigh" if (j, a) == (GROUP - 1, PACKS - 1) else None)
            pt.free = [ev]
            if g == 0:
                st["ot"] = ot.take()
            o = st["ot"]
            view = s.mem[:, 0:GROUP * (DL + 1)].rearrange("p (j d) -> p j d", j=GROUP)
            dve.wait(ev, *o.before)
            dve.wait(dve.do(lambda e: e.reciprocal(m.mem[:, 1, :], view[:, :, DL]), "recip"))
            dst = o.mem[:, :, :].rearrange("p (pair two) d -> p two pair d", two=2)[:, parity, first:first + GROUP, :]
            o.ready = tt(dve, dst, view[:, :, 0:DL],
                         m.mem[:, 1, :].unsqueeze(2).to_broadcast([P, GROUP, DL]), ALU.mult, stage="o")
            s.free = [o.ready]
            m.free = [o.ready]
            if g == GROUPS - 1:
                v.free = [ev]

        def turn_out(n, part):
            l, b, t = where(n)
            o = state[n]["ot"]
            if t == 0 and part == 0:
                batch[l, b] = {"oT": oT.take()}
            d = batch[l, b]["oT"]
            z = turned.take()
            pe.wait(*z.before, o.ready)
            for j in range(4):
                two = slice(part * 8 + 2 * j, part * 8 + 2 * j + 2)
                ev = turn(z.mem[:, j * P:(j + 1) * P], o.mem[:, two, :], stage="oT" if j == 3 else None)
            act.wait(ev, *d.before)
            d.ready = copy(d.mem[:, part * 4:part * 4 + 4, t * P:(t + 1) * P],
                           z.mem[:, :].rearrange("p (j t) -> p j t", j=4), "oT")
            z.free = [d.ready]
            if part == 1:
                o.free = [ev]

        def finish(l, b):
            w, col = layer_w[l], cl[l % 2]
            d = batch[l, b]["oT"]

            def columns(lo, n=1):
                return col[:, lo:lo + n]
            s = proj.take()
            pe.wait(*s.before, d.ready)
            for j in range(PAIRS):
                ev = mm(s.mem[:, :], w.mem[:, W_O + j * D:W_O + (j + 1) * D], d.mem[:, j, :], start=j == 0,
                        stop=j == PAIRS - 1, stage="wo" if j == PAIRS - 1 else None)
            d.free = [ev]
            dve.wait(ev, *xs_of[l, b].read)
            r_ev = tt(dve, xT[:, b, :], s.mem[:, :], xT[:, b, :], ALU.add, stage="res")
            s.free = [r_ev]
            f = xf.take()
            pool.wait(r_ev, *f.before)
            f_ev = shifted(f.mem, b, "xf")
            yield
            z = turn_tiles(lambda t: f.mem[:, t * P:(t + 1) * P], [f_ev], "xf_tok")
            f.free = [z.ready]
            dve.wait(z.ready)
            n_ev = layer_norm(xn, z.mem[:, :].rearrange("p (t d) -> p t d", t=TILES), "xn")
            z.free = [n_ev]
            yield
            z = turn_tiles(lambda t: xn[:, t, :], [n_ev], "xnT")
            dve.wait(z.ready)
            act.wait(z.ready, w.ready2)
            xn_ev = activate(xnT[:, :], z.mem[:, :], ACT.Identity, "xnT", scale=columns(C_G), bias=columns(C_B))
            z.free = [xn_ev]
            yield
            h = hT.take()
            for c in range(GLUC):
                s = proj.take()
                pe.wait(*s.before, xn_ev)
                ev = mm(s.mem[:, :], w.mem[:, W_1 + GLUP + c * P:W_1 + GLUP + (c + 1) * P], xnT[:, :], stage="w1")
                g = glu.take()
                act.wait(ev, *g.before)
                g_ev = activate(g.mem[:, :], s.mem[:, :], ACT.Gelu, "gelu", bias=columns(C_B1 + GLUC + c))
                s.free = [g_ev]
                s = proj.take()
                pe.wait(*s.before)
                ev = mm(s.mem[:, :], w.mem[:, W_1 + c * P:W_1 + (c + 1) * P], xnT[:, :], stage="w1")
                dve.wait(ev, g_ev, *h.before)
                h_ev = stt(h.mem[:, c, :], s.mem[:, :], columns(C_B1 + c), g.mem[:, :], ALU.add, ALU.mult, stage="hT")
                s.free = [h_ev]
                g.free = [h_ev]
            act.wait(ev)
            yield
            s = proj.take()
            pe.wait(*s.before, h_ev)
            for c in range(GLUC):
                ev = mm(s.mem[:, :], w.mem[:, W_2 + c * D:W_2 + (c + 1) * D], h.mem[:, c, :], start=c == 0,
                        stop=c == GLUC - 1, stage="w2" if c == GLUC - 1 else None)
            h.free = [ev]
            dve.wait(ev, f_ev)
            x_ev[b] = stt(xT[:, b, :], s.mem[:, :], columns(C_B2), xT[:, b, :], ALU.add, ALU.add, stage="x")
            s.free = [x_ev[b]]
            dve.wait(x_ev[b])
            if b == SEQS - 1:
                w.free = [ev, x_ev[b]]
                if l + 2 < DEPTH:
                    layer_w[l + 2] = load_layer(l + 2)
            yield
            if l == DEPTH - 1:
                f = xf.take()
                dve.wait(*f.before)
                a_ev = tt(dve, f.mem[:, :], xT[:, b, :], x3T[:, b, :], ALU.add, stage="last_sum")
                z = turn_tiles(lambda t: f.mem[:, t * P:(t + 1) * P], [a_ev], "last_tok")
                dve.wait(z.ready)
                last = f.mem[:, :].rearrange("p (t d) -> p t d", t=TILES)
                n_ev = layer_norm(last, z.mem[:, :].rearrange("p (t d) -> p t d", t=TILES), "last_ln")
                z.free = [n_ev]
                sp.wait(n_ev)
                f.free = [load(io["out"][b].rearrange("(t p) d -> p t d", p=P), last, "store")]
                out_ev[:] = f.free

        pending = []
        START = 3 * GROUPS
        for G in range(-START, TOTAL * GROUPS + 8):
            if pending and G % 2 == 0:
                if next(pending[0], "end") == "end":
                    pending.pop(0)
            if G + START < TOTAL * GROUPS:
                project((G + START) // GROUPS, (G + START) % GROUPS)
                l, b, t = where((G + START) // GROUPS)
                if (G + START) % GROUPS == 0 and t == 0:
                    xs_of[l, b].read = [xs_of[l, b].ready]
            if 0 <= G + GROUPS < TOTAL * GROUPS:
                project_v((G + GROUPS) // GROUPS, (G + GROUPS) % GROUPS)
                rotate((G + GROUPS) // GROUPS, (G + GROUPS) % GROUPS)
            if 0 <= G < TOTAL * GROUPS:
                score(G // GROUPS, G % GROUPS)
            if 0 <= G - 1 < TOTAL * GROUPS:
                turn_prob((G - 1) // GROUPS, (G - 1) % GROUPS)
            if 0 <= G - 2 < TOTAL * GROUPS:
                weigh((G - 2) // GROUPS, (G - 2) % GROUPS)
            if G >= 6 and (G - 6) % GROUPS < 2 and (G - 6) // GROUPS < TOTAL:
                n = (G - 6) // GROUPS
                turn_out(n, (G - 6) % GROUPS)
                if (G - 6) % GROUPS == 1:
                    state.pop(n - 1, None)
                    if where(n)[2] == TILES - 1:
                        pending.append(finish(*where(n)[:2]))
        while pending:
            if next(pending[0], "end") == "end":
                pending.pop(0)
        sp.wait(*out_ev)

        block = ctx.enter_context(nc.Block())

        @block.sync
        def _(e):
            sp.play(e)

        @block.tensor
        def _(e):
            pe.play(e)

        @block.scalar
        def _(e):
            act.play(e)

        @block.vector
        def _(e):
            dve.play(e)

        @block.gpsimd
        def _(e):
            pool.play(e)


def shape_constants():
    f = np.float32
    c = {"ident": np.eye(P, dtype=f)}
    i = np.arange(P)
    c["causal"] = np.where(i[None, :] > i[:, None], f(MASKED), f(0))
    q, k = i % PACK, np.arange(KEYS)
    ok = (k[None, :] >= q[:, None]) & (k[None, :] <= q[:, None] + WINDOW)
    ok0 = ok & ~((i[:, None] < PACK) & (k[None, :] < WINDOW))
    band = np.stack([ok, ok0], 1)[:, :, None, :].repeat(GROUP, 2)
    c["band"] = np.where(band, f(0), f(MASKED))

    def tiles(a):
        return np.ascontiguousarray(a.reshape(TILES, P, -1).transpose(1, 0, 2))
    t = np.arange(TOKENS, dtype=f)
    inv = f(1.0) / np.power(f(10000.0), np.arange(0, DH, 2, dtype=f) / f(DH))
    fr = np.concatenate([t[:, None] * inv] * 2, 1).astype(f)
    sgn = np.where(np.arange(DH) < DH // 2, f(-1), f(1))
    c["rope"] = np.stack([tiles(np.cos(fr)), tiles(np.sin(fr) * sgn)], 1)
    half = np.arange(0, DL, 2, dtype=f)
    inv = f(1.0) / np.power(f(10000.0), half / f(DL))
    fr = np.concatenate([t[:, None] * inv] * 2, 1).astype(f)
    bs = (half + f(0.4 * DL)) / f(1.4 * DL)
    power = (t - f(TOKENS // 2)) / f(WINDOW // 2)
    s = np.power(bs[None, :], power[:, None]).astype(f)
    s = np.concatenate([s, s], 1)
    sgn = np.where(np.arange(DL) < DL // 2, f(-1), f(1))
    r = f(1.0) / s
    c["base"] = np.stack([tiles(np.cos(fr) * s), tiles(np.sin(fr) * sgn * s),
                          tiles(np.cos(fr) * r), tiles(np.sin(fr) * sgn * r)], 1)
    return {k: np.ascontiguousarray(v) for k, v in c.items()}


def kernel(**inputs):
    import concourse.bacc as _bacc
    from concourse.bass_utils import run_bass_kernel_spmd as _run

    g = {k: np.asarray(v) for k, v in inputs.items()}
    a = shape_constants()
    x = g["L0_attn_x"]

    def rows(v):
        return np.broadcast_to(v[None], (P,) + v.shape)

    def padded(v, axis, n):
        shape = list(v.shape)
        shape[axis] = n - shape[axis]
        return np.concatenate([v, np.zeros(shape, v.dtype)], axis)

    a["x0T"] = x.transpose(2, 0, 1)
    a["x0"] = x.reshape(SEQS, TILES, P, D).transpose(0, 2, 1, 3)
    a["w_in"] = g["L0_attn_W_in"].T
    a["w_out"] = g["L0_attn_W_out"].T
    a["ccols"] = np.concatenate([g["L0_attn_conv_w"][:, 0, :], g["L0_attn_conv_b"][:, None],
                                 g["L0_attn_a_param"][:, None]], 1)
    a["lnrow"] = rows(np.stack([g["L0_attn_ln_w"], g["L0_attn_ln_b"]]))
    a["rw"] = g["L0_ffn_router_W"]
    a["rrow"] = rows(np.stack([g["L0_ffn_router_b"], np.arange(EXPERTS, 0, -1, dtype=np.float32)]))
    a["w1"] = g["L0_ffn_W1"].transpose(1, 0, 2)
    a["w2"] = g["L0_ffn_W2"].reshape(EXPERTS, FFC, P, D).transpose(2, 0, 1, 3)
    a["b1"] = g["L0_ffn_b1"].reshape(EXPERTS, FFC, P).transpose(2, 0, 1)
    a["b2"] = g["L0_ffn_b2"]
    a["wqkv"] = np.concatenate([g["L1_attn_Wq"], g["L1_attn_Wk"], g["L1_attn_Wv"]], 1)
    a["wo"] = g["L1_attn_Wo"].reshape(HQ, DH, D).transpose(1, 0, 2)
    w1 = g["L1_ffn_W1"]
    b1 = g["L1_ffn_b1"]
    wo = g["L1_ffn_Wo"].reshape(DEPTH, PAIRS, P, D).transpose(0, 2, 1, 3).reshape(DEPTH, P, PAIRS * D)
    w2 = padded(g["L1_ffn_W2"], 1, GLUP).reshape(DEPTH, GLUC, P, D).transpose(0, 2, 1, 3).reshape(DEPTH, P, GLUC * D)
    a["wl"] = np.concatenate([g["L1_ffn_Wqkv"], wo, padded(w1[:, :, :GLU], 2, GLUP),
                              padded(w1[:, :, GLU:], 2, GLUP), w2], 2)
    cols = np.concatenate([padded(b1[:, :GLU], 1, GLUP), padded(b1[:, GLU:], 1, GLUP)], 1)
    a["cl"] = np.concatenate([g["L1_ffn_ln_g"][:, :, None], g["L1_ffn_ln_b"][:, :, None],
                              g["L1_ffn_b2"][:, :, None],
                              cols.reshape(DEPTH, 2 * GLUC, P).transpose(0, 2, 1)], 2)
    half = DL // 2
    qs, ks = g["L1_ffn_q_scale"], g["L1_ffn_k_scale"]

    def swap(v):
        return np.concatenate([v[:, half:], v[:, :half]], 1)
    row = np.stack([qs, swap(qs), ks, swap(ks)], 1)
    a["qkrow"] = np.broadcast_to(row[:, None], (DEPTH, P) + row.shape[1:])

    nc = _bacc.Bacc("TRN2", target_bir_lowering=False, num_devices=1)
    arrays, io = {}, {}
    for name, v in a.items():
        v = np.ascontiguousarray(v)
        arrays[f"in_{name}"] = v
        ap = nc.dram_tensor(f"in_{name}", v.shape, mybir.dt.from_np(v.dtype), kind="ExternalInput").ap()
        io[name] = ap
    io["out"] = nc.dram_tensor("out_0", (SEQS, TOKENS, D), F32, kind="ExternalOutput").ap()
    build(nc, io)
    r = _run(nc, [arrays], core_ids=[0])
    return r.results[0]["out_0"]
```

```python
from contextlib import ExitStack

import numpy as np

import concourse.bass as bass
from concourse import mybir

F32 = mybir.dt.float32
BF16 = mybir.dt.bfloat16
I32 = mybir.dt.int32
ALU = mybir.AluOpType
ACT = mybir.ActivationFunctionType
AX_X = mybir.AxisListType.X

P = 128
SEQS, TOKENS, D = 4, 512, 128
TILES = TOKENS // P
LN_EPS = 1e-5

TAPS = 5
EXPERTS, FF = 8, 512
FFC = FF // P

HQ, HKV, DH = 8, 4, 128

DEPTH, HEADS, DL = 6, 16, 64
INNER = HEADS * DL
PAIRS = HEADS // 2
WINDOW = 32
PACK = 64
PACKS = P // PACK
KEYS = PACK + WINDOW
QK_SCALE = 8.0
GLU = int(D * 4 * 2 / 3)
GLUC = -(-GLU // P)
GLUP = GLUC * P
GROUP = 4
MASKED = -(2.0 ** 120)

W_QKV, W_O, W_1, W_2 = 0, 3 * INNER, 3 * INNER + PAIRS * D, 3 * INNER + PAIRS * D + 2 * GLUP
W_ALL = W_2 + GLUC * D
C_G, C_B, C_B2, C_B1 = 0, 1, 2, 3
C_ALL = 3 + 2 * GLUC
RSQRT_SEED = float(0x5F3759DF)


class Event:
    def __init__(self, sem, value):
        self.sem, self.value = sem, value


class Lane:

    def __init__(self, name, new_sem):
        self.name, self.new_sem = name, new_sem
        self.steps, self.sems, self.counts, self.waited = [], {}, {}, {}

    def wait(self, *events):
        for ev in events:
            if ev is None or self.waited.get(ev.sem, 0) >= ev.value:
                continue
            self.waited[ev.sem] = ev.value
            self.steps.append(lambda e, ev=ev: e.wait_ge(ev.sem, ev.value))

    def do(self, build, stage=None, by=1):
        if stage is None:
            self.steps.append(build)
            return None
        if stage not in self.sems:
            self.sems[stage] = self.new_sem(f"{self.name}_{stage}")
            self.counts[stage] = 0
        self.counts[stage] += by
        sem = self.sems[stage]
        self.steps.append(lambda e: build(e).then_inc(sem, by))
        return Event(sem, self.counts[stage])

    def play(self, e):
        for step in self.steps:
            step(e)


class Slot:

    def __init__(self, mem):
        self.mem, self.free, self.before, self.ready = mem, [], [], None


class Ring:
    def __init__(self, mems):
        self.slots, self.at = [Slot(m) for m in mems], 0

    def take(self):
        s = self.slots[self.at % len(self.slots)]
        self.at += 1
        assert s.free is not None, "taken again before its readers were queued"
        s.before, s.free = s.free, None
        return s


def build(nc, io):
    ctx = ExitStack()
    with ctx:
        def new_sem(name):
            return ctx.enter_context(nc.semaphore(name))

        def sb(name, shape, dt=F32, stack=None):
            return (stack or ctx).enter_context(nc.sbuf_tensor(name, shape, dt))

        pe, act, dve = Lane("pe", new_sem), Lane("act", new_sem), Lane("dve", new_sem)
        pool, sp = Lane("pool", new_sem), Lane("sp", new_sem)

        def load(dst, src, name):
            return sp.do(lambda e: e.dma_start(dst, src), name, 16)

        def mm(out, lhsT, rhs, start=True, stop=True, stage=None):
            return pe.do(lambda e: e.matmul(out, lhsT, rhs, start=start, stop=stop, skip_group_check=True), stage)

        def turn(out, in_, start=True, stop=True, stage=None):
            ident_ = ident[0:in_.shape[0], 0:in_.shape[0]]
            return pe.do(lambda e: e.matmul(out, in_, ident_, start=start, stop=stop, is_transpose=True,
                                            skip_group_check=True), stage)

        def activate(out, in_, func, stage, **kw):
            return act.do(lambda e: e.activation(out, in_, func, **kw), stage)

        def copy(out, in_, stage):
            return act.do(lambda e: e.activation(out, in_, ACT.Copy), stage)

        def tt(lane, out, a, b, op, stage=None):
            return lane.do(lambda e: e.tensor_tensor(out, a, b, op), stage)

        def ts(out, a, s1, s2, op0, op1=None, stage=None):
            if op1 is None:
                return dve.do(lambda e: e.tensor_scalar(out, a, s1, None, op0), stage)
            return dve.do(lambda e: e.tensor_scalar(out, a, s1, s2, op0, op1), stage)

        def stt(out, a, s, b, op0, op1, stage=None):
            return dve.do(lambda e: e.scalar_tensor_tensor(out=out, in0=a, scalar=s, in1=b, op0=op0, op1=op1), stage)

        def reduce(out, a, op, stage=None, negate=False):
            return dve.do(lambda e: e.tensor_reduce(out, a, AX_X, op, negate=negate), stage)

        def recip(out, a, stage=None):
            return dve.do(lambda e: e.reciprocal(out, a), stage)

        def chained(ev):
            dve.wait(ev)
            return ev

        banks = [ctx.enter_context(nc.psum_tensor(f"bank{i}", [P, 512], F32)) for i in range(8)]
        proj, scores, turned, summed = (Ring(banks[i:i + 2]) for i in (0, 2, 4, 6))

        ident = sb("ident", [P, P])
        identb = sb("identb", [P, P], BF16)
        band = sb("band", [P, 2, GROUP, KEYS], BF16)
        causal = sb("causal", [P, P], BF16)
        xT = sb("xT", [P, SEQS, TOKENS])
        x3T = sb("x3T", [P, SEQS, TOKENS])
        wl = Ring([sb("wl0", [P, W_ALL])])
        cl = [sb(f"cl{i}", [P, C_ALL]) for i in range(2)]
        stats = sb("stats", [P, TILES, 6])
        moments = sb("moments", [P, TILES, 2])
        rstd = sb("rstd", [P, TILES])
        nw = sb("nw", [P, 3, 32])

        c_ev = load(ident[:, :], io["ident"], "const")
        pe.wait(c_ev)

        def inverse_root(out, src, guard, op):
            n = src.shape[-1] if len(src.shape) == 2 else src.shape[1]
            x, y, t = (nw[:, i, 0:n] for i in range(3))
            chained(ts(x, src, guard, None, op, stage="newton"))
            chained(ts(t.bitcast(I32), x.bitcast(I32), 1, None, ALU.arith_shift_right, stage="newton"))
            chained(ts(y.bitcast(I32), t.bitcast(I32), -1.0, RSQRT_SEED, ALU.mult, ALU.add, stage="newton"))
            for k in range(3):
                chained(stt(t, y, -0.5, y, ALU.mult, ALU.mult, stage="newton"))
                chained(tt(dve, t, t, x, ALU.mult, stage="newton"))
                to = y if k < 2 else out
                ev = chained(stt(to, t, 1.5, y, ALU.add, ALU.mult, stage="newton"))
            return ev

        def layer_norm(dst, src, stage):
            for t in range(TILES):
                ev = dve.do(lambda e, t=t: e.bn_stats(stats[:, t, :], src[:, t, :]), "bn_stats")
            chained(ev)
            for t in range(TILES):
                ev = dve.do(lambda e, t=t: e.bn_aggr(moments[:, t, :], stats[:, t, :]), "bn_aggr")
            chained(ev)
            inverse_root(rstd[:, :], moments[:, :, 1], LN_EPS, ALU.add)
            for t in range(TILES):
                ev = ts(dst[:, t, :], src[:, t, :], moments[:, t, 0:1], rstd[:, t:t + 1],
                        ALU.subtract, ALU.mult, stage=stage)
            return ev

        def turn_tiles(src, events, stage):
            s = turned.take()
            pe.wait(*s.before, *events)
            for t in range(TILES):
                ev = turn(s.mem[:, t * P:(t + 1) * P], src(t), stage=stage if t == TILES - 1 else None)
            s.ready = ev
            return s

        def load_layer(l):
            w = wl.take()
            sp.wait(*w.before)
            w.ready = load(w.mem[:, :], io["wl"][l], f"weights{l % 2}")
            w.ready2 = load(cl[l % 2][:, :], io["cl"][l], f"columns{l % 2}")
            return w

        early = ExitStack()
        with early:
            def eb(name, shape, dt=F32):
                return sb(name, shape, dt, early)

            x0T = xT
            x0 = Ring([eb(f"x0_{i}", [P, TILES, D]) for i in range(2)])
            w_in = eb("w_in", [P, 2 * D])
            w_out = eb("w_out", [P, D])
            ccols = eb("ccols", [P, TAPS + 2])
            lnrow = eb("lnrow", [P, 2, D])
            rw = eb("rw", [P, EXPERTS])
            rrow = eb("rrow", [P, 2, EXPERTS])
            w1 = eb("w1", [P, EXPERTS, FF])
            w2 = eb("w2", [P, EXPERTS, FFC, D])
            b1 = eb("b1", [P, EXPERTS, FFC])
            b2 = eb("b2", [EXPERTS, D])
            wqkv = eb("wqkv", [P, (HQ + 2 * HKV) * DH])
            wo = eb("wo", [P, HQ, D])
            rope = eb("rope", [P, 2, TILES, DH])

            band32 = eb("band32", [P, 2, GROUP, KEYS])
            causal32 = eb("causal32", [P, P])
            load(band32[:, :, :, :], io["band"], "masks")
            masks_ev = load(causal32[:, :], io["causal"], "masks")
            act.wait(c_ev, masks_ev)
            copy(identb[:, :], ident[:, :], "masks")
            copy(band[:, :, :, :], band32[:, :, :, :], "masks")
            pe.wait(copy(causal[:, :], causal32[:, :], "masks"))

            io_ev = {}
            for dst, name in ((x0T, "x0T"), (w_in, "w_in"), (ccols, "ccols"), (w_out, "w_out"),
                              (lnrow, "lnrow"), (rw, "rw"), (rrow, "rrow"), (w1, "w1"), (b1, "b1"), (b2, "b2"),
                              (w2, "w2"), (wqkv, "wqkv"), (rope, "rope"), (wo, "wo")):
                full = dst[tuple(slice(None) for _ in dst.shape)]
                io_ev[name] = load(full, io[name], "load_" + name)

            gate = eb("gate", [P, TOKENS])
            val = eb("val", [P, TOKENS + TAPS - 1])
            conv = eb("conv", [P, TOKENS])
            y = eb("y", [P, TOKENS])
            resT = eb("resT", [P, TOKENS])
            tokA = eb("tokA", [P, TILES, D])
            x1 = eb("x1", [P, TILES, D])
            x1T = eb("x1T", [P, TOKENS])
            decay = eb("decay", [P, 1])

            edge_ev = dve.do(lambda e: e.memset(val[:, :], 0.0), "edges")
            act.wait(io_ev["ccols"])
            decay_ev = activate(decay[:, :], ccols[:, TAPS + 1:TAPS + 2], ACT.Tanh, "decay")
            act.wait(edge_ev)
            dve.wait(decay_ev)

            free = {k: [] for k in ("gate", "val", "y", "resT", "x1T", "x1", "x2T", "h")}
            x1_ev, x1T_ev = None, None

            def load_x0(b):
                s = x0.take()
                sp.wait(*s.before)
                s.ready = load(s.mem[:, :, :], io["x0"][b], f"x0_{b % 2}")
                return s

            x0_tok = {0: load_x0(0), 1: load_x0(1)}

            def gated_scan(b):
                sg = proj.take()
                pe.wait(*sg.before, io_ev["x0T"], io_ev["w_in"])
                g_ev = mm(sg.mem[:, :], w_in[:, 0:D], x0T[:, b, :], stage="gate")
                sv = proj.take()
                pe.wait(*sv.before)
                v_ev = mm(sv.mem[:, :], w_in[:, D:2 * D], x0T[:, b, :], stage="val")
                act.wait(g_ev, *free["gate"])
                sig_ev = activate(gate[:, :], sg.mem[:, :], ACT.Sigmoid, "sigmoid")
                sg.free = [sig_ev]
                act.wait(v_ev, *free["val"])
                val_ev = copy(val[:, TAPS // 2:TAPS // 2 + TOKENS], sv.mem[:, :], "val")
                sv.free = [val_ev]
                dve.wait(val_ev, io_ev["ccols"])
                chained(ts(conv[:, :], val[:, 0:TOKENS], ccols[:, 0:1], ccols[:, TAPS:TAPS + 1],
                           ALU.mult, ALU.add, stage="conv"))
                for k in range(1, TAPS):
                    ev = chained(stt(conv[:, :], val[:, k:k + TOKENS], ccols[:, k:k + 1], conv[:, :],
                                     ALU.mult, ALU.add, stage="conv"))
                free["val"] = [ev]
                dve.wait(sig_ev)
                ev = chained(tt(dve, conv[:, :], conv[:, :], gate[:, :], ALU.mult, stage="conv"))
                free["gate"] = [ev]
                dve.wait(*free["y"])
                scan_ev = dve.do(lambda e: e.tensor_tensor_scan(
                    y[:, :], decay[:, 0:1].to_broadcast([P, TOKENS]), conv[:, :], 0.0, ALU.mult, ALU.add), "scan")
                so = proj.take()
                pe.wait(*so.before, scan_ev, io_ev["w_out"])
                o_ev = mm(so.mem[:, :], w_out[:, :], y[:, :], stage="w_out")
                free["y"] = [o_ev]
                dve.wait(o_ev, *free["resT"], scan_ev)
                res_ev = tt(dve, resT[:, :], so.mem[:, :], x0T[:, b, :], ALU.add, stage="res")
                so.free = [res_ev]
                s = turn_tiles(lambda t: resT[:, t * P:(t + 1) * P], [res_ev], "res_tok")
                free["resT"] = [s.ready]
                dve.wait(s.ready)
                ln_ev = layer_norm(tokA, s.mem[:, :].rearrange("p (t d) -> p t d", t=TILES), "ln0")
                s.free = [ln_ev]
                dve.wait(ln_ev, io_ev["lnrow"], x0_tok[b].ready)
                chained(tt(dve, tokA[:, :, :], tokA[:, :, :], lnrow[:, 0:1, :].to_broadcast([P, TILES, D]),
                           ALU.mult, stage="affine"))
                chained(tt(dve, tokA[:, :, :], tokA[:, :, :], lnrow[:, 1:2, :].to_broadcast([P, TILES, D]),
                           ALU.add, stage="affine"))
                ev = chained(tt(dve, tokA[:, :, :], tokA[:, :, :], x0_tok[b].mem[:, :, :], ALU.add, stage="affine"))
                x0_tok[b].free = [ev]
                if b + 2 < SEQS:
                    x0_tok[b + 2] = load_x0(b + 2)
                dve.wait(*free["x1"])
                x1_ev = layer_norm(x1, tokA, "x1")
                s = turn_tiles(lambda t: x1[:, t, :], [x1_ev], "x1T")
                act.wait(s.ready, *free["x1T"])
                x1T_ev = copy(x1T[:, :], s.mem[:, :], "x1T")
                s.free = [x1T_ev]
                return x1_ev, x1T_ev

            lg = eb("lg", [P, TILES, EXPERTS])
            pr = eb("pr", [P, TILES, EXPERTS])
            rowst = eb("rowst", [P, 4, TILES])
            gates = eb("gates", [P, TILES, EXPERTS])
            gatesT = eb("gatesT", [EXPERTS, TOKENS])
            hbuf = Ring([eb(f"hbuf{i}", [P, FFC, TOKENS]) for i in range(2)])
            acc = eb("acc", [P, TILES, D])
            x2T = eb("x2T", [P, TOKENS])

            def per_tile(col):
                return col.unsqueeze(2).to_broadcast([P, TILES, EXPERTS])

            def router(x1T_ev, x1_ev):
                s = proj.take()
                pe.wait(*s.before, x1T_ev, io_ev["rw"])
                for t in range(TILES):
                    ev = mm(s.mem[:, t * EXPERTS:(t + 1) * EXPERTS], x1T[:, t * P:(t + 1) * P], rw[:, :],
                            stage="logits" if t == TILES - 1 else None)
                dve.wait(ev, io_ev["rrow"])
                ev = chained(tt(dve, lg[:, :, :], s.mem[:, 0:TILES * EXPERTS].rearrange("p (t e) -> p t e", t=TILES),
                                rrow[:, 0:1, :].to_broadcast([P, TILES, EXPERTS]), ALU.add, stage="router"))
                s.free = [ev]
                chained(reduce(rowst[:, 0, :], lg[:, :, :], ALU.max, stage="router"))
                ev = chained(tt(dve, lg[:, :, :], lg[:, :, :], per_tile(rowst[:, 0, :]), ALU.subtract, stage="router"))
                act.wait(ev)
                ev = activate(pr[:, :, :], lg[:, :, :], ACT.Exp, "router_exp")
                dve.wait(ev)
                chained(reduce(rowst[:, 1, :], pr[:, :, :], ALU.add, stage="router"))
                chained(recip(rowst[:, 2, :], rowst[:, 1, :], stage="router"))
                chained(tt(dve, pr[:, :, :], pr[:, :, :], per_tile(rowst[:, 2, :]), ALU.mult, stage="router"))
                chained(reduce(rowst[:, 0, :], pr[:, :, :], ALU.max, stage="router"))
                chained(tt(dve, lg[:, :, :], pr[:, :, :], per_tile(rowst[:, 0, :]), ALU.is_equal, stage="router"))
                chained(tt(dve, lg[:, :, :], lg[:, :, :], rrow[:, 1:2, :].to_broadcast([P, TILES, EXPERTS]),
                           ALU.mult, stage="router"))
                chained(reduce(rowst[:, 3, :], lg[:, :, :], ALU.max, stage="router"))
                chained(tt(dve, lg[:, :, :], lg[:, :, :], per_tile(rowst[:, 3, :]), ALU.is_equal, stage="router"))
                g_ev = chained(tt(dve, gates[:, :, :], lg[:, :, :], pr[:, :, :], ALU.mult, stage="router"))
                s = turned.take()
                pe.wait(*s.before, g_ev)
                for t in range(TILES):
                    ev = turn(s.mem[0:EXPERTS, t * P:(t + 1) * P], gates[:, t, :],
                              stage="gatesT" if t == TILES - 1 else None)
                act.wait(ev)
                gT_ev = copy(gatesT[:, :], s.mem[0:EXPERTS, :], "gatesT")
                s.free = [gT_ev]
                s = proj.take()
                pe.wait(*s.before, gT_ev, io_ev["b2"])
                for t in range(TILES):
                    ev = mm(s.mem[:, t * D:(t + 1) * D], gatesT[:, t * P:(t + 1) * P], b2[:, :],
                            stage="gate_b2" if t == TILES - 1 else None)
                dve.wait(ev, x1_ev)
                ev = chained(tt(dve, acc[:, :, :], s.mem[:, :].rearrange("p (t d) -> p t d", t=TILES), x1[:, :, :],
                                ALU.add, stage="acc"))
                s.free = [ev]
                return ev

            def experts(x1T_ev):
                def up(e_):
                    h = hbuf.take()
                    for c in range(FFC):
                        s = proj.take()
                        pe.wait(*s.before, x1T_ev, io_ev["w1"])
                        ev = mm(s.mem[:, :], w1[:, e_, c * P:(c + 1) * P], x1T[:, :], stage="up")
                        act.wait(ev, *h.before, io_ev["b1"])
                        s.free = [activate(h.mem[:, c, :], s.mem[:, :], ACT.Relu, "relu", bias=b1[:, e_, c:c + 1])]
                        h.ready = s.free[0]
                    return h

                def down(e_, h):
                    s = summed.take()
                    pe.wait(*s.before, h.ready, io_ev["w2"])
                    for t in range(TILES):
                        for c in range(FFC):
                            ev = mm(s.mem[:, t * D:(t + 1) * D], h.mem[:, c, t * P:(t + 1) * P], w2[:, e_, c, :],
                                    start=c == 0, stop=c == FFC - 1,
                                    stage="down" if (t, c) == (TILES - 1, FFC - 1) else None)
                    h.free = [ev]
                    dve.wait(ev)
                    for t in range(TILES):
                        ev = stt(acc[:, t, :], s.mem[:, t * D:(t + 1) * D], gates[:, t, e_:e_ + 1], acc[:, t, :],
                                 ALU.mult, ALU.add, stage="acc")
                    s.free = [ev]
                    dve.wait(ev)
                    return ev

                last = up(0)
                for e_ in range(1, EXPERTS):
                    nxt = up(e_)
                    down(e_ - 1, last)
                    last = nxt
                return down(EXPERTS - 1, last)

            prod = Ring([eb(f"prod{i}", [P, 2, GROUP, DH]) for i in range(2)])
            q2T = eb("q2T", [P, HQ, TOKENS])
            k2T = eb("k2T", [P, HKV, TOKENS])
            v2 = eb("v2", [P, TILES, HKV * DH])
            prob2 = Ring([eb(f"prob2{i}", [P, TOKENS]) for i in range(3)])
            prob2T = Ring([eb(f"prob2T{i}", [P, TILES, P]) for i in range(2)])
            soft2 = Ring([eb(f"soft2{i}", [P, 4]) for i in range(4)])
            o2 = eb("o2", [P, HQ, DH])
            o2T = Ring([eb(f"o2T{i}", [P, HQ, P]) for i in range(2)])
            free.update({"q2T": [], "k2T": [], "v2": [], "o2": []})
            scale2 = 1.0 / float(np.sqrt(np.float32(DH)))

            def qkv2(x2T_ev):
                half = DH // 2
                for t in range(TILES):
                    for c in range(4):
                        s = proj.take()
                        pe.wait(*s.before, x2T_ev, io_ev["wqkv"])
                        ev = mm(s.mem[:, :], x2T[:, t * P:(t + 1) * P], wqkv[:, c * 512:(c + 1) * 512], stage="qkv2")
                        if c == 3:
                            act.wait(ev, *free["v2"])
                            v_ev = copy(v2[:, t, :], s.mem[:, :], "v2")
                            s.free = [v_ev]
                            continue
                        w = prod.take()
                        dve.wait(ev, *w.before, io_ev["rope"])
                        src = s.mem[:, :].rearrange("p (h d) -> p h d", h=GROUP)

                        def table(k, lo, hi):
                            return rope[:, k, t, lo:hi].unsqueeze(1).to_broadcast([P, GROUP, hi - lo])
                        tt(dve, w.mem[:, 0, :, :], src, table(0, 0, DH), ALU.mult)
                        tt(dve, w.mem[:, 1, :, 0:half], src[:, :, half:DH], table(1, 0, half), ALU.mult)
                        r_ev = tt(dve, w.mem[:, 1, :, half:DH], src[:, :, 0:half], table(1, half, DH), ALU.mult,
                                  stage="rope2")
                        s.free = [r_ev]
                        z = turned.take()
                        pe.wait(*z.before, r_ev)
                        for j in range(GROUP):
                            turn(z.mem[:, j * P:(j + 1) * P], w.mem[:, 0, j, :], stop=False)
                            ev = turn(z.mem[:, j * P:(j + 1) * P], w.mem[:, 1, j, :], start=False,
                                      stage="rope2T" if j == GROUP - 1 else None)
                        w.free = [ev]
                        dst = (q2T[:, c * GROUP:(c + 1) * GROUP, t * P:(t + 1) * P] if c < 2
                               else k2T[:, :, t * P:(t + 1) * P])
                        act.wait(ev, *free["q2T"], *free["k2T"])
                        qk_ev = copy(dst, z.mem[:, :].rearrange("p (j t) -> p j t", j=GROUP), "qk2T")
                        z.free = [qk_ev]
                return qk_ev, v_ev

            def attend2(qk_ev, v_ev, x2T_ev):
                work = [(t, h) for t in range(TILES) for h in range(HQ)]
                kept = {}

                def score(t, h):
                    n = (t + 1) * P
                    s = scores.take()
                    pe.wait(*s.before, qk_ev)
                    mm(s.mem[:, 0:n], q2T[:, h, t * P:(t + 1) * P], k2T[:, h // 2, 0:n], stop=False)
                    ev = mm(s.mem[:, n - P:n], identb[:, :], causal[:, :], start=False, stage="score2")
                    m, p = soft2.take(), prob2.take()
                    dve.wait(ev, *m.before)
                    chained(reduce(m.mem[:, 0:1], s.mem[:, 0:n], ALU.max, stage="max2"))
                    b_ev = ts(m.mem[:, 1:2], m.mem[:, 0:1], -scale2, None, ALU.mult, stage="max2")
                    act.wait(b_ev, *p.before)
                    e_ev = activate(p.mem[:, 0:n], s.mem[:, 0:n], ACT.Exp, "exp2", scale=scale2,
                                    bias=m.mem[:, 1:2], accum_out=m.mem[:, 2:3])
                    s.free = [e_ev]
                    kept[t, h] = (m, p, e_ev)

                def weigh(t, h):
                    m, p, e_ev = kept.pop((t, h))
                    z = turned.take()
                    pe.wait(*z.before, e_ev)
                    for k in range(t + 1):
                        ev = turn(z.mem[:, k * P:(k + 1) * P], p.mem[:, k * P:(k + 1) * P],
                                  stage="prob2T" if k == t else None)
                    p.free = [ev]
                    q = prob2T.take()
                    act.wait(ev, *q.before)
                    c_ev = copy(q.mem[:, 0:t + 1, :], z.mem[:, 0:(t + 1) * P].rearrange("p (k q) -> p k q", q=P),
                                "prob2T")
                    z.free = [c_ev]
                    o = summed.take()
                    pe.wait(*o.before, c_ev, v_ev)
                    for k in range(t + 1):
                        ev = mm(o.mem[:, 0:DH], q.mem[:, k, :], v2[:, k, (h // 2) * DH:(h // 2 + 1) * DH],
                                start=k == 0, stop=k == t, stage="pv2" if k == t else None)
                    q.free = [ev]
                    if h == 0:
                        dve.wait(*free["o2"])
                    dve.wait(e_ev)
                    chained(recip(m.mem[:, 3:4], m.mem[:, 2:3], stage="norm2"))
                    dve.wait(ev)
                    n_ev = ts(o2[:, h, :], o.mem[:, 0:DH], m.mem[:, 3:4], None, ALU.mult, stage="norm2")
                    o.free = [n_ev]
                    m.free = [n_ev]
                    if h == HQ - 1:
                        d = o2T.take()
                        for g in range(HQ // GROUP):
                            z = turned.take()
                            pe.wait(*z.before, n_ev)
                            for j in range(GROUP):
                                ev = turn(z.mem[:, j * P:(j + 1) * P], o2[:, g * GROUP + j, :],
                                          stage="o2T" if j == GROUP - 1 else None)
                            act.wait(ev, *d.before)
                            z.free = [copy(d.mem[:, g * GROUP:(g + 1) * GROUP, :],
                                           z.mem[:, :].rearrange("p (j t) -> p j t", j=GROUP), "o2T")]
                            d.ready = z.free[0]
                        free["o2"] = [ev]
                        s = proj.take()
                        pe.wait(*s.before, d.ready, io_ev["wo"])
                        for k in range(HQ):
                            ev = mm(s.mem[:, 0:P], wo[:, k, :], d.mem[:, k, :], start=k == 0, stop=k == HQ - 1,
                                    stage="wo2" if k == HQ - 1 else None)
                        d.free = [ev]
                        dve.wait(ev, x2T_ev, *free["resT"])
                        r_ev = tt(dve, resT[:, t * P:(t + 1) * P], s.mem[:, 0:P], x2T[:, t * P:(t + 1) * P],
                                  ALU.add, stage="res")
                        s.free = [r_ev]
                        return r_ev
                    return None

                for i in range(len(work) + 1):
                    if i < len(work):
                        score(*work[i])
                    if i:
                        ev = weigh(*work[i - 1])
                free["q2T"] = free["k2T"] = free["v2"] = [Event(pe.sems["pv2"], pe.counts["pv2"])]
                return ev

            def sequence(b):
                x1_ev, x1T_ev = gated_scan(b)
                router(x1T_ev, x1_ev)
                acc_ev = experts(x1T_ev)
                free["x1"] = [acc_ev]
                free["x1T"] = [Event(pe.sems["up"], pe.counts["up"])]
                dve.wait(acc_ev)
                ln_ev = layer_norm(tokA, acc, "x2")
                s = turn_tiles(lambda t: tokA[:, t, :], [ln_ev], "x2T")
                dve.wait(s.ready)
                act.wait(s.ready, *free["x2T"])
                x2T_ev = copy(x2T[:, :], s.mem[:, :], "x2T")
                s.free = [x2T_ev]
                qk_ev, v_ev = qkv2(x2T_ev)
                r_ev = attend2(qk_ev, v_ev, x2T_ev)
                free["x2T"] = [r_ev]
                s = turn_tiles(lambda t: resT[:, t * P:(t + 1) * P], [r_ev], "res2_tok")
                free["resT"] = [s.ready]
                dve.wait(s.ready)
                ln_ev = layer_norm(tokA, s.mem[:, :].rearrange("p (t d) -> p t d", t=TILES), "x3")
                s.free = [ln_ev]
                s = turn_tiles(lambda t: tokA[:, t, :], [ln_ev], "x3T")
                dve.wait(s.ready)
                act.wait(s.ready)
                copy(xT[:, b, :], s.mem[:, :], "x3T")
                ev = copy(x3T[:, b, :], s.mem[:, :], "x3T")
                s.free = [ev]
                return ev

            layer_w = {0: load_layer(0)}
            x3_ev = [sequence(b) for b in range(SEQS)]

        ends = []
        for src in (pe, act, dve):
            ends += [Event(src.sems[k], src.counts[k]) for k in src.sems]
        for lane in (pe, act, dve, pool, sp):
            lane.wait(*ends)

        summed, slow = Ring(banks[6:7]), Ring(banks[7:8])
        wl.slots.append(Slot(sb("wl1", [P, W_ALL])))
        wl.at = 1
        base = sb("base", [P, 4, TILES, DL])
        table = sb("table", [P, 4, TILES, DL])
        qkrow = [sb(f"qkrow{i}", [P, 4, DL]) for i in range(2)]
        base_ev = load(base[:, :, :, :], io["base"], "base")

        xs = Ring([sb(f"xs{i}", [P, WINDOW + TOKENS]) for i in range(2)])
        xf = Ring([sb("xf0", [P, TOKENS])])
        raw = Ring([sb(f"raw{i}", [P, 2 * HEADS, DL]) for i in range(3)])
        sq = Ring([sb(f"sq{i}", [P, 8, DL]) for i in range(2)])
        rot = Ring([sb(f"rot{i}", [P, 8, DL]) for i in range(3)])
        n2 = Ring([sb(f"n2{i}", [P, 2 * HEADS]) for i in range(2)])
        rn = Ring([sb(f"rn{i}", [P, 2 * HEADS]) for i in range(2)])
        qT = Ring([sb(f"qT{i}", [P, PAIRS, P]) for i in range(2)])
        kT = Ring([sb(f"kT{i}", [P, PAIRS, WINDOW + P]) for i in range(3)])
        vp = Ring([sb(f"vp{i}", [KEYS, PACKS, HEADS, DL + 1]) for i in range(3)])
        soft = Ring([sb(f"soft{i}", [P, 2, GROUP]) for i in range(4)])
        prob = Ring([sb(f"prob{i}", [P, GROUP, KEYS]) for i in range(3)])
        probT = Ring([sb(f"probT{i}", [KEYS, GROUP, P]) for i in range(2)])
        ot = Ring([sb(f"ot{i}", [P, HEADS, DL]) for i in range(2)])
        oT = Ring([sb("oT0", [P, PAIRS, TOKENS])])
        xn = sb("xn", [P, TILES, D])
        xnT = sb("xnT", [P, TOKENS])
        glu = Ring([sb(f"glu{i}", [P, TOKENS]) for i in range(2)])
        hT = Ring([sb("hT0", [P, GLUC, TOKENS])])

        TOTAL = DEPTH * SEQS * TILES
        GROUPS = HEADS // GROUP
        x_ev = list(x3_ev)
        xs_of, tab_ev, tab_free = {}, {}, {0: [], 1: [], "last": []}
        state = {}
        batch = {}
        out_ev = []

        def where(n):
            return n // (SEQS * TILES), n // TILES % SEQS, n % TILES

        last_pool = [None]

        def on_pool(build_, stage):
            pool.wait(last_pool[0])
            last_pool[0] = pool.do(build_, stage)
            return last_pool[0]

        def unit(x, inverse):
            return on_pool(lambda e: e.tensor_tensor(x, x, inverse, ALU.mult), "unit")

        def shifted(dst, b, stage):
            on_pool(lambda e: e.memset(dst[D // 2:D, 0:1], 0.0), stage)
            on_pool(lambda e: e.tensor_copy(dst[0:D // 2, :], xT[0:D // 2, b, :]), stage)
            return on_pool(lambda e: e.tensor_copy(dst[D // 2:D, 1:TOKENS], xT[D // 2:D, b, 0:TOKENS - 1]), stage)

        for s in xs.slots:
            ones_ev = on_pool(lambda e, s=s: e.memset(s.mem[:, 0:WINDOW + 1], 0.0), "fill")
        for s in vp.slots:
            ones_ev = on_pool(lambda e, s=s: e.memset(s.mem[:, :, :, DL:DL + 1], 1.0), "fill")
        pe.wait(ones_ev)
        act.wait(ones_ev)
        pool.wait(ones_ev)

        def tables(l):
            row = qkrow[l % 2]
            sp.wait(*tab_free[l % 2])
            r_ev = load(row[:, :, :], io["qkrow"][l], f"qkrow{l % 2}")
            dve.wait(r_ev, base_ev, *tab_free["last"])
            for k in range(4):
                ev = tt(dve, table[:, k, :, :], base[:, k, :, :],
                        row[:, k:k + 1, :].to_broadcast([P, TILES, DL]), ALU.mult, stage="tables")
            tab_ev[l] = ev

        def qk_pe(n, part):
            l, b, t = where(n)
            if part == 0:
                if t == 0:
                    s = xs.take()
                    pool.wait(*s.before, x_ev[b])
                    s.ready = shifted(s.mem[:, WINDOW:WINDOW + TOKENS], b, "xs")
                    xs_of[l, b] = s
                state[n] = {"raw": raw.take(), "n2": n2.take(), "rn": rn.take()}
            s, w = xs_of[l, b], layer_w[l]
            bank = proj.take()
            pe.wait(*bank.before, s.ready, w.ready)
            bank.ready = mm(bank.mem[:, :], s.mem[:, WINDOW + t * P:WINDOW + (t + 1) * P],
                            w.mem[:, part * 512:(part + 1) * 512], stage="qk")
            state[n]["qk", part] = bank

        def qk_act(n, part):
            st = state[n]
            bank, q = st.pop(("qk", part)), sq.take()
            src = bank.mem[:, :].rearrange("p (h d) -> p h d", d=DL)
            act.wait(bank.ready, *q.before, *st["raw"].before)
            q.ready = activate(q.mem[:, :, :], src, ACT.Square, "square")
            bank.free = [copy(st["raw"].mem[:, part * 8:(part + 1) * 8, :], src, "raw")]
            st["sq", part], st["raw_ev"] = q, bank.free[0]

        def norm_dve(n, part):
            st = state[n]
            q = st.pop(("sq", part))
            dve.wait(q.ready, *st["n2"].before)
            n_ev = reduce(st["n2"].mem[:, part * 8:(part + 1) * 8], q.mem[:, :, :], ALU.add, stage="norm2sum")
            q.free = [n_ev]
            if part == 3:
                dve.wait(n_ev, *st["rn"].before)
                r_ev = inverse_root(st["rn"].mem[:, :], st["n2"].mem[:, :], 1e-24, ALU.max)
                st["n2"].free = [r_ev]
                pool.wait(r_ev, st["raw_ev"])
                r = st["raw"]
                r.unit = []
                for h in range(4):
                    hs = slice(h * 8, (h + 1) * 8)
                    r.unit.append(unit(r.mem[:, hs, :], st["rn"].mem[:, hs].unsqueeze(2).to_broadcast([P, 8, DL])))
                st["rn"].free = [r.unit[-1]]

        def v_pe(n, part):
            l, b, t = where(n)
            st, s, w = state[n], xs_of[l, b], layer_w[l]
            if part == 0:
                st["vp"] = vp.take()
            a, half = part // 2, part % 2
            bank = proj.take()
            pe.wait(*bank.before, s.ready, w.ready)
            bank.ready = mm(bank.mem[0:KEYS, :], s.mem[:, t * P + a * PACK:t * P + a * PACK + KEYS],
                            w.mem[:, 2 * INNER + half * 512:2 * INNER + (half + 1) * 512], stage="v")
            st["v", part] = bank
            if t == TILES - 1 and part == 3:
                s.free = [bank.ready]

        def v_act(n, part):
            st = state[n]
            a, half = part // 2, part % 2
            bank = st.pop(("v", part))
            act.wait(bank.ready, *st["vp"].before)
            bank.free = [copy(st["vp"].mem[:, a, half * 8:(half + 1) * 8, 0:DL],
                              bank.mem[0:KEYS, :].rearrange("p (h d) -> p h d", d=DL), "v")]
            st["vp"].ready = bank.free[0]

        def rotate_dve(n, part):
            l, b, t = where(n)
            st = state[n]
            if part == 0:
                if n % (SEQS * TILES) == 0:
                    tables(l)
                    if l == 0:
                        layer_w[1] = load_layer(1)
            r, v = st["raw"], rot.take()
            hs = slice(part * 8, (part + 1) * 8)
            which = 0 if part < 2 else 2
            half = DL // 2

            def tab(k, lo, hi):
                return table[:, k, t, lo:hi].unsqueeze(1).to_broadcast([P, 8, hi - lo])
            dve.wait(r.unit[part], tab_ev[l], *v.before)
            tt(dve, v.mem[:, :, 0:half], r.mem[:, hs, half:DL], tab(which + 1, 0, half), ALU.mult)
            ev = tt(dve, v.mem[:, :, half:DL], r.mem[:, hs, 0:half], tab(which + 1, half, DL), ALU.mult,
                    stage="rot_sin")
            dve.wait(ev)
            v.ready = tt(dve, r.mem[:, hs, :], r.mem[:, hs, :], tab(which, 0, DL), ALU.mult, stage="rot_cos")
            if n % (SEQS * TILES) == SEQS * TILES - 1:
                tab_free.update({l % 2: [v.ready], "last": [v.ready]})
            st["rot", part] = v

        def rotate_pe(n, part):
            st = state[n]
            v, r = st.pop(("rot", part)), st["raw"]
            z = turned.take()
            pe.wait(*z.before, v.ready)
            for j in range(4):
                turn(z.mem[:, j * P:(j + 1) * P], r.mem[:, part * 8 + 2 * j:part * 8 + 2 * j + 2, :], stop=False)
                ev = turn(z.mem[:, j * P:(j + 1) * P], v.mem[:, 2 * j:2 * j + 2, :], start=False,
                          stage="qkT" if j == 3 else None)
            z.ready = ev
            v.free = [ev]
            if part == 3:
                r.free = [ev]
            st["qkT", part] = z

        def rotate_act(n, part):
            l, b, t = where(n)
            st = state[n]
            if part == 0:
                st["qT"], st["kT"] = qT.take(), kT.take()
                k = st["kT"]
                if t == 0:
                    pool.wait(*k.before)
                    k.edge = on_pool(lambda e: e.memset(k.mem[:, :, 0:WINDOW], 0.0), "kT_edge")
            z = st.pop(("qkT", part))
            ps = slice((part % 2) * 4, (part % 2) * 4 + 4)
            src = z.mem[:, :].rearrange("p (j t) -> p j t", j=4)
            if part < 2:
                q = st["qT"]
                act.wait(z.ready, *q.before)
                q.ready = copy(q.mem[:, ps, :], src, "qT")
                z.free = [q.ready]
            else:
                k = st["kT"]
                act.wait(z.ready, *k.before)
                k.ready = copy(k.mem[:, ps, WINDOW:WINDOW + P], src, "kT")
                z.free = [k.ready]
            if part == 3 and t < TILES - 1:
                nxt = kT.slots[kT.at % len(kT.slots)]
                k = st["kT"]
                pool.wait(k.ready, *nxt.free)
                nxt.edge = on_pool(lambda e: e.tensor_copy(nxt.mem[:, :, 0:WINDOW], k.mem[:, :, P:P + WINDOW]),
                                   "kT_edge")
                st["edge_copied"] = nxt.edge

        def heads_of(g):
            return g % 2, 4 * (g // 2)

        def score_pe(n, g):
            l, b, t = where(n)
            st = state[n]
            q, k = st["qT"], st["kT"]
            parity, first = heads_of(g)
            s = scores.take()
            pe.wait(*s.before, q.ready, k.ready, k.edge)
            mm(s.mem[:, 0:GROUP * KEYS], identb[:, :], band[:, 1 if t == 0 else 0, :, :], stop=False)
            rows = slice(parity * DL, (parity + 1) * DL)
            for j in range(GROUP):
                for a in range(PACKS):
                    ev = mm(s.mem[a * PACK:(a + 1) * PACK, j * KEYS:(j + 1) * KEYS],
                            q.mem[rows, first + j, a * PACK:(a + 1) * PACK],
                            k.mem[rows, first + j, a * PACK:a * PACK + KEYS], start=False,
                            stage="score" if (j, a) == (GROUP - 1, PACKS - 1) else None)
            if g == GROUPS - 1:
                q.free, k.free = [ev], [ev, st.get("edge_copied")]
            s.ready = ev
            st["score", g] = s

        def soft_dve(n, g):
            st = state[n]
            s, m, p = st.pop(("score", g)), soft.take(), prob.take()
            view = s.mem[:, 0:GROUP * KEYS].rearrange("p (j k) -> p j k", j=GROUP)
            dve.wait(s.ready, *m.before, *p.before)
            dve.wait(reduce(m.mem[:, 0, :], view, ALU.max, stage="max"))
            p.ready = tt(dve, p.mem[:, :, :], view, m.mem[:, 0, :].unsqueeze(2).to_broadcast([P, GROUP, KEYS]),
                         ALU.subtract, stage="less_max")
            s.free = [p.ready]
            st["soft", g] = (m, p)

        def exp_act(n, g):
            m, p = state[n]["soft", g]
            act.wait(p.ready)
            p.ready = activate(p.mem[:, :, :], p.mem[:, :, :], ACT.Exp, "exp", scale=QK_SCALE)

        def prob_pe(n, g):
            st = state[n]
            m, p = st["soft", g]
            z = turned.take()
            pe.wait(*z.before, p.ready)
            for j in range(GROUP):
                ev = turn(z.mem[0:KEYS, j * P:(j + 1) * P], p.mem[:, j, :], stage="probT" if j == GROUP - 1 else None)
            p.free, z.ready = [ev], ev
            st["probT", g] = z

        def prob_act(n, g):
            st = state[n]
            z, pt = st.pop(("probT", g)), probT.take()
            act.wait(z.ready, *pt.before)
            pt.ready = copy(pt.mem[:, :, :], z.mem[0:KEYS, :].rearrange("p (j q) -> p j q", j=GROUP), "probT")
            z.free = [pt.ready]
            st["pt", g] = pt

        def weigh_pe(n, g):
            st = state[n]
            pt, v = st.pop(("pt", g)), st["vp"]
            parity, first = heads_of(g)
            s = summed.take()
            pe.wait(*s.before, pt.ready, v.ready)
            for j in range(GROUP):
                head = 2 * (first + j) + parity
                for a in range(PACKS):
                    ev = mm(s.mem[a * PACK:(a + 1) * PACK, j * (DL + 1):(j + 1) * (DL + 1)],
                            pt.mem[:, j, a * PACK:(a + 1) * PACK], v.mem[:, a, head, :],
                            stage="weigh" if (j, a) == (GROUP - 1, PACKS - 1) else None)
            pt.free, s.ready = [ev], ev
            st["sum", g] = s
            if g == GROUPS - 1:
                v.free = [ev]

        def divide_dve(n, g):
            st = state[n]
            s, (m, p) = st.pop(("sum", g)), st.pop(("soft", g))
            parity, first = heads_of(g)
            if g == 0:
                st["ot"] = ot.take()
            o = st["ot"]
            view = s.mem[:, 0:GROUP * (DL + 1)].rearrange("p (j d) -> p j d", j=GROUP)
            dve.wait(s.ready, *o.before)
            dve.wait(recip(m.mem[:, 1, :], view[:, :, DL], stage="recip"))
            dst = o.mem[:, :, :].rearrange("p (pair two) d -> p two pair d", two=2)[:, parity, first:first + GROUP, :]
            o.ready = tt(dve, dst, view[:, :, 0:DL],
                         m.mem[:, 1, :].unsqueeze(2).to_broadcast([P, GROUP, DL]), ALU.mult, stage="o")
            s.free, m.free = [o.ready], [o.ready]

        def out_pe(n, part):
            o = state[n]["ot"]
            z = turned.take()
            pe.wait(*z.before, o.ready)
            for j in range(4):
                two = slice(part * 8 + 2 * j, part * 8 + 2 * j + 2)
                ev = turn(z.mem[:, j * P:(j + 1) * P], o.mem[:, two, :], stage="oT" if j == 3 else None)
            z.ready = ev
            state[n]["oT", part] = z
            if part == 1:
                o.free = [ev]

        def out_act(n, part):
            l, b, t = where(n)
            if t == 0 and part == 0:
                batch[l, b] = {"oT": oT.take()}
            d, z = batch[l, b]["oT"], state[n].pop(("oT", part))
            act.wait(z.ready, *d.before)
            d.ready = copy(d.mem[:, part * 4:part * 4 + 4, t * P:(t + 1) * P],
                           z.mem[:, :].rearrange("p (j t) -> p j t", j=4), "oT")
            z.free = [d.ready]

        def finish(l, b):
            w, col = layer_w[l], cl[l % 2]
            d = batch[l, b]["oT"]

            def columns(lo, n=1):
                return col[:, lo:lo + n]

            def turn_slow(src, events, stage):
                z = slow.take()
                pe.wait(*z.before, *events)
                for t in range(TILES):
                    z.ready = turn(z.mem[:, t * P:(t + 1) * P], src(t), stage=stage if t == TILES - 1 else None)
                return z
            s = slow.take()
            pe.wait(*s.before, d.ready)
            for j in range(PAIRS):
                ev = mm(s.mem[:, :], w.mem[:, W_O + j * D:W_O + (j + 1) * D], d.mem[:, j, :], start=j == 0,
                        stop=j == PAIRS - 1, stage="wo" if j == PAIRS - 1 else None)
                if j == PAIRS // 2 - 1:
                    yield
            d.free = [ev]
            yield
            dve.wait(ev, xs_of[l, b].ready)
            r_ev = tt(dve, xT[:, b, :], s.mem[:, :], xT[:, b, :], ALU.add, stage="res")
            s.free = [r_ev]
            f = xf.take()
            pool.wait(r_ev, *f.before)
            f_ev = shifted(f.mem, b, "xf")
            yield
            yield
            z = turn_slow(lambda t: f.mem[:, t * P:(t + 1) * P], [f_ev], "xf_tok")
            f.free = [z.ready]
            yield
            dve.wait(z.ready)
            n_ev = layer_norm(xn, z.mem[:, :].rearrange("p (t d) -> p t d", t=TILES), "xn")
            z.free = [n_ev]
            yield
            z = turn_slow(lambda t: xn[:, t, :], [n_ev], "xnT")
            dve.wait(z.ready)
            act.wait(z.ready, w.ready2)
            xn_ev = activate(xnT[:, :], z.mem[:, :], ACT.Identity, "xnT", scale=columns(C_G), bias=columns(C_B))
            z.free = [xn_ev]
            h = hT.take()
            for c in range(GLUC):
                yield
                s = proj.take()
                pe.wait(*s.before, xn_ev)
                ev = mm(s.mem[:, :], w.mem[:, W_1 + GLUP + c * P:W_1 + GLUP + (c + 1) * P], xnT[:, :], stage="w1")
                g = glu.take()
                act.wait(ev, *g.before)
                g_ev = activate(g.mem[:, :], s.mem[:, :], ACT.Gelu, "gelu", bias=columns(C_B1 + GLUC + c))
                s.free = [g_ev]
                s = slow.take()
                pe.wait(*s.before)
                ev = mm(s.mem[:, :], w.mem[:, W_1 + c * P:W_1 + (c + 1) * P], xnT[:, :], stage="w1")
                dve.wait(ev, g_ev, *h.before)
                h_ev = stt(h.mem[:, c, :], s.mem[:, :], columns(C_B1 + c), g.mem[:, :], ALU.add, ALU.mult, stage="hT")
                s.free = [h_ev]
                g.free = [h_ev]
            act.wait(ev)
            yield
            s = slow.take()
            pe.wait(*s.before, h_ev)
            for c in range(GLUC):
                ev = mm(s.mem[:, :], w.mem[:, W_2 + c * D:W_2 + (c + 1) * D], h.mem[:, c, :], start=c == 0,
                        stop=c == GLUC - 1, stage="w2" if c == GLUC - 1 else None)
            h.free = [ev]
            yield
            dve.wait(ev, f_ev)
            x_ev[b] = stt(xT[:, b, :], s.mem[:, :], columns(C_B2), xT[:, b, :], ALU.add, ALU.add, stage="x")
            s.free = [x_ev[b]]
            dve.wait(x_ev[b])
            if b == SEQS - 1:
                w.free = [ev, x_ev[b]]
                if l + 2 < DEPTH:
                    layer_w[l + 2] = load_layer(l + 2)
            if l == DEPTH - 1:
                yield
                f = xf.take()
                dve.wait(*f.before)
                a_ev = tt(dve, f.mem[:, :], xT[:, b, :], x3T[:, b, :], ALU.add, stage="last_sum")
                yield
                z = turn_slow(lambda t: f.mem[:, t * P:(t + 1) * P], [a_ev], "last_tok")
                yield
                dve.wait(z.ready)
                last = f.mem[:, :].rearrange("p (t d) -> p t d", t=TILES)
                n_ev = layer_norm(last, z.mem[:, :].rearrange("p (t d) -> p t d", t=TILES), "last_ln")
                z.free = [n_ev]
                sp.wait(n_ev)
                f.free = [load(io["out"][b].rearrange("(t p) d -> p t d", p=P), last, "store")]
                out_ev[:] = f.free

        pending = []
        QUARTERS = TOTAL * GROUPS
        AHEAD, ROT, VAL = 3 * GROUPS, GROUPS + 2, GROUPS

        def at(stage, i):
            if 0 <= i < QUARTERS:
                stage(i // GROUPS, i % GROUPS)

        for G in range(-AHEAD, QUARTERS + 12):
            at(score_pe, G)
            at(exp_act, G - 1)
            at(qk_pe, G + AHEAD)
            at(norm_dve, G + AHEAD - 1)
            at(rotate_dve, G + ROT)
            at(soft_dve, G)
            at(qk_act, G + AHEAD)
            at(v_pe, G + VAL)
            at(v_act, G + VAL)
            at(rotate_pe, G + ROT - 1)
            at(rotate_act, G + ROT - 1)
            at(weigh_pe, G - 2)
            at(divide_dve, G - 2)
            at(prob_pe, G - 1)
            at(prob_act, G - 1)
            i = G - 6
            if i >= 0 and i % GROUPS < 2 and i < QUARTERS:
                at(out_pe, i)
                at(out_act, i)
                n = i // GROUPS
                if i % GROUPS == 1:
                    state.pop(n, None)
                    if where(n)[2] == TILES - 1:
                        pending.append(finish(*where(n)[:2]))
            if pending and next(pending[0], "end") == "end":
                pending.pop(0)
        while pending:
            if next(pending[0], "end") == "end":
                pending.pop(0)
        sp.wait(*out_ev)

        block = ctx.enter_context(nc.Block())

        @block.sync
        def _(e):
            sp.play(e)

        @block.tensor
        def _(e):
            pe.play(e)

        @block.scalar
        def _(e):
            act.play(e)

        @block.vector
        def _(e):
            dve.play(e)

        @block.gpsimd
        def _(e):
            pool.play(e)


def shape_constants():
    f = np.float32
    c = {"ident": np.eye(P, dtype=f)}
    i = np.arange(P)
    c["causal"] = np.where(i[None, :] > i[:, None], f(MASKED), f(0))
    q, k = i % PACK, np.arange(KEYS)
    ok = (k[None, :] >= q[:, None]) & (k[None, :] <= q[:, None] + WINDOW)
    ok0 = ok & ~((i[:, None] < PACK) & (k[None, :] < WINDOW))
    band = np.stack([ok, ok0], 1)[:, :, None, :].repeat(GROUP, 2)
    c["band"] = np.where(band, f(0), f(MASKED))

    def tiles(a):
        return np.ascontiguousarray(a.reshape(TILES, P, -1).transpose(1, 0, 2))
    t = np.arange(TOKENS, dtype=f)
    inv = f(1.0) / np.power(f(10000.0), np.arange(0, DH, 2, dtype=f) / f(DH))
    fr = np.concatenate([t[:, None] * inv] * 2, 1).astype(f)
    sgn = np.where(np.arange(DH) < DH // 2, f(-1), f(1))
    c["rope"] = np.stack([tiles(np.cos(fr)), tiles(np.sin(fr) * sgn)], 1)
    half = np.arange(0, DL, 2, dtype=f)
    inv = f(1.0) / np.power(f(10000.0), half / f(DL))
    fr = np.concatenate([t[:, None] * inv] * 2, 1).astype(f)
    bs = (half + f(0.4 * DL)) / f(1.4 * DL)
    power = (t - f(TOKENS // 2)) / f(WINDOW // 2)
    s = np.power(bs[None, :], power[:, None]).astype(f)
    s = np.concatenate([s, s], 1)
    sgn = np.where(np.arange(DL) < DL // 2, f(-1), f(1))
    r = f(1.0) / s
    c["base"] = np.stack([tiles(np.cos(fr) * s), tiles(np.sin(fr) * sgn * s),
                          tiles(np.cos(fr) * r), tiles(np.sin(fr) * sgn * r)], 1)
    return {k: np.ascontiguousarray(v) for k, v in c.items()}


def kernel(**inputs):
    import concourse.bacc as _bacc
    from concourse.bass_utils import run_bass_kernel_spmd as _run

    g = {k: np.asarray(v) for k, v in inputs.items()}
    a = shape_constants()
    x = g["L0_attn_x"]

    def rows(v):
        return np.broadcast_to(v[None], (P,) + v.shape)

    def padded(v, axis, n):
        shape = list(v.shape)
        shape[axis] = n - shape[axis]
        return np.concatenate([v, np.zeros(shape, v.dtype)], axis)

    a["x0T"] = x.transpose(2, 0, 1)
    a["x0"] = x.reshape(SEQS, TILES, P, D).transpose(0, 2, 1, 3)
    a["w_in"] = g["L0_attn_W_in"].T
    a["w_out"] = g["L0_attn_W_out"].T
    a["ccols"] = np.concatenate([g["L0_attn_conv_w"][:, 0, :], g["L0_attn_conv_b"][:, None],
                                 g["L0_attn_a_param"][:, None]], 1)
    a["lnrow"] = rows(np.stack([g["L0_attn_ln_w"], g["L0_attn_ln_b"]]))
    a["rw"] = g["L0_ffn_router_W"]
    a["rrow"] = rows(np.stack([g["L0_ffn_router_b"], np.arange(EXPERTS, 0, -1, dtype=np.float32)]))
    a["w1"] = g["L0_ffn_W1"].transpose(1, 0, 2)
    a["w2"] = g["L0_ffn_W2"].reshape(EXPERTS, FFC, P, D).transpose(2, 0, 1, 3)
    a["b1"] = g["L0_ffn_b1"].reshape(EXPERTS, FFC, P).transpose(2, 0, 1)
    a["b2"] = g["L0_ffn_b2"]
    a["wqkv"] = np.concatenate([g["L1_attn_Wq"], g["L1_attn_Wk"], g["L1_attn_Wv"]], 1)
    a["wo"] = g["L1_attn_Wo"].reshape(HQ, DH, D).transpose(1, 0, 2)
    w1 = g["L1_ffn_W1"]
    b1 = g["L1_ffn_b1"]
    wo = g["L1_ffn_Wo"].reshape(DEPTH, PAIRS, P, D).transpose(0, 2, 1, 3).reshape(DEPTH, P, PAIRS * D)
    w2 = padded(g["L1_ffn_W2"], 1, GLUP).reshape(DEPTH, GLUC, P, D).transpose(0, 2, 1, 3).reshape(DEPTH, P, GLUC * D)
    a["wl"] = np.concatenate([g["L1_ffn_Wqkv"], wo, padded(w1[:, :, :GLU], 2, GLUP),
                              padded(w1[:, :, GLU:], 2, GLUP), w2], 2)
    cols = np.concatenate([padded(b1[:, :GLU], 1, GLUP), padded(b1[:, GLU:], 1, GLUP)], 1)
    a["cl"] = np.concatenate([g["L1_ffn_ln_g"][:, :, None], g["L1_ffn_ln_b"][:, :, None],
                              g["L1_ffn_b2"][:, :, None],
                              cols.reshape(DEPTH, 2 * GLUC, P).transpose(0, 2, 1)], 2)
    half = DL // 2
    qs, ks = g["L1_ffn_q_scale"], g["L1_ffn_k_scale"]

    def swap(v):
        return np.concatenate([v[:, half:], v[:, :half]], 1)
    row = np.stack([qs, swap(qs), ks, swap(ks)], 1)
    a["qkrow"] = np.broadcast_to(row[:, None], (DEPTH, P) + row.shape[1:])

    nc = _bacc.Bacc("TRN2", target_bir_lowering=False, num_devices=1)
    arrays, io = {}, {}
    for name, v in a.items():
        v = np.ascontiguousarray(v)
        arrays[f"in_{name}"] = v
        ap = nc.dram_tensor(f"in_{name}", v.shape, mybir.dt.from_np(v.dtype), kind="ExternalInput").ap()
        io[name] = ap
    io["out"] = nc.dram_tensor("out_0", (SEQS, TOKENS, D), F32, kind="ExternalOutput").ap()
    build(nc, io)
    r = _run(nc, [arrays], core_ids=[0])
    return r.results[0]["out_0"]
```

```python
from contextlib import ExitStack

import numpy as np

import concourse.bass as bass
from concourse import mybir

F32 = mybir.dt.float32
BF16 = mybir.dt.bfloat16
I32 = mybir.dt.int32
ALU = mybir.AluOpType
ACT = mybir.ActivationFunctionType
AX_X = mybir.AxisListType.X

P = 128
SEQS, TOKENS, D = 4, 512, 128
TILES = TOKENS // P
LN_EPS = 1e-5

TAPS = 5
EXPERTS, FF = 8, 512
FFC = FF // P

HQ, HKV, DH = 8, 4, 128

DEPTH, HEADS, DL = 6, 16, 64
INNER = HEADS * DL
PAIRS = HEADS // 2
WINDOW = 32
PACK = 64
PACKS = P // PACK
KEYS = PACK + WINDOW
QK_SCALE = 8.0
GLU = int(D * 4 * 2 / 3)
GLUC = -(-GLU // P)
GLUP = GLUC * P
GROUP = 4
MASKED = -(2.0 ** 120)

W_QKV, W_O, W_1, W_2 = 0, 3 * INNER, 3 * INNER + PAIRS * D, 3 * INNER + PAIRS * D + 2 * GLUP
W_ALL = W_2 + GLUC * D
C_G, C_B, C_B2, C_B1 = 0, 1, 2, 3
C_ALL = 3 + 2 * GLUC
RSQRT_SEED = float(0x5F3759DF)


class Event:
    def __init__(self, sem, value):
        self.sem, self.value = sem, value


class Lane:

    def __init__(self, name, new_sem):
        self.name, self.new_sem = name, new_sem
        self.steps, self.sems, self.counts, self.waited = [], {}, {}, {}

    def wait(self, *events):
        for ev in events:
            if ev is None or self.waited.get(ev.sem, 0) >= ev.value:
                continue
            self.waited[ev.sem] = ev.value
            self.steps.append(lambda e, ev=ev: e.wait_ge(ev.sem, ev.value))

    def do(self, build, stage=None, by=1):
        if stage is None:
            self.steps.append(build)
            return None
        if stage not in self.sems:
            self.sems[stage] = self.new_sem(f"{self.name}_{stage}")
            self.counts[stage] = 0
        self.counts[stage] += by
        sem = self.sems[stage]
        self.steps.append(lambda e: build(e).then_inc(sem, by))
        return Event(sem, self.counts[stage])

    def play(self, e):
        for step in self.steps:
            step(e)


class Slot:

    def __init__(self, mem):
        self.mem, self.free, self.before, self.ready = mem, [], [], None


class Ring:
    def __init__(self, mems):
        self.slots, self.at = [Slot(m) for m in mems], 0

    def take(self):
        s = self.slots[self.at % len(self.slots)]
        self.at += 1
        assert s.free is not None, "taken again before its readers were queued"
        s.before, s.free = s.free, None
        return s


def build(nc, io):
    ctx = ExitStack()
    with ctx:
        def new_sem(name):
            return ctx.enter_context(nc.semaphore(name))

        def sb(name, shape, dt=F32, stack=None):
            return (stack or ctx).enter_context(nc.sbuf_tensor(name, shape, dt))

        pe, act, dve = Lane("pe", new_sem), Lane("act", new_sem), Lane("dve", new_sem)
        pool, sp = Lane("pool", new_sem), Lane("sp", new_sem)

        def load(dst, src, name):
            return sp.do(lambda e: e.dma_start(dst, src), name, 16)

        def mm(out, lhsT, rhs, start=True, stop=True, stage=None):
            return pe.do(lambda e: e.matmul(out, lhsT, rhs, start=start, stop=stop, skip_group_check=True), stage)

        def turn(out, in_, start=True, stop=True, stage=None):
            ident_ = ident[0:in_.shape[0], 0:in_.shape[0]]
            return pe.do(lambda e: e.matmul(out, in_, ident_, start=start, stop=stop, is_transpose=True,
                                            skip_group_check=True), stage)

        def activate(out, in_, func, stage, **kw):
            return act.do(lambda e: e.activation(out, in_, func, **kw), stage)

        def copy(out, in_, stage):
            return act.do(lambda e: e.activation(out, in_, ACT.Copy), stage)

        def tt(lane, out, a, b, op, stage=None):
            return lane.do(lambda e: e.tensor_tensor(out, a, b, op), stage)

        def ts(out, a, s1, s2, op0, op1=None, stage=None):
            if op1 is None:
                return dve.do(lambda e: e.tensor_scalar(out, a, s1, None, op0), stage)
            return dve.do(lambda e: e.tensor_scalar(out, a, s1, s2, op0, op1), stage)

        def stt(out, a, s, b, op0, op1, stage=None):
            return dve.do(lambda e: e.scalar_tensor_tensor(out=out, in0=a, scalar=s, in1=b, op0=op0, op1=op1), stage)

        def reduce(out, a, op, stage=None, negate=False):
            return dve.do(lambda e: e.tensor_reduce(out, a, AX_X, op, negate=negate), stage)

        def recip(out, a, stage=None):
            return dve.do(lambda e: e.reciprocal(out, a), stage)

        def chained(ev):
            dve.wait(ev)
            return ev

        banks = [ctx.enter_context(nc.psum_tensor(f"bank{i}", [P, 512], F32)) for i in range(8)]
        proj, scores, turned = (Ring(banks[i:i + 2]) for i in (0, 2, 4))
        summed, slow = Ring(banks[6:7]), Ring(banks[7:8])

        ident = sb("ident", [P, P])
        identb = sb("identb", [P, P], BF16)
        band = sb("band", [P, 2, GROUP, KEYS], BF16)
        causal = sb("causal", [P, P], BF16)
        xT = sb("xT", [P, SEQS, TOKENS])
        x3T = sb("x3T", [P, SEQS, TOKENS])
        wl = Ring([sb("wl0", [P, W_ALL])])
        cl = [sb(f"cl{i}", [P, C_ALL]) for i in range(2)]
        stats = sb("stats", [P, TILES, 6])
        moments = sb("moments", [P, TILES, 2])
        rstd = sb("rstd", [P, TILES])
        nw = sb("nw", [P, 3, 32])
        nw_ln = sb("nw_ln", [P, 3, TILES])

        c_ev = load(ident[:, :], io["ident"], "const")
        pe.wait(c_ev)

        def root_steps(out, src, guard, op, rows, done):
            n = src.shape[-1] if len(src.shape) == 2 else src.shape[1]
            x, y, t = (rows[:, i, 0:n] for i in range(3))
            steps = [lambda: ts(x, src, guard, None, op, stage="newton"),
                     lambda: ts(t.bitcast(I32), x.bitcast(I32), 1, None, ALU.arith_shift_right, stage="newton"),
                     lambda: ts(y.bitcast(I32), t.bitcast(I32), -1.0, RSQRT_SEED, ALU.mult, ALU.add, stage="newton")]
            for k in range(3):
                steps.append(lambda: stt(t, y, -0.5, y, ALU.mult, ALU.mult, stage="newton"))
                steps.append(lambda: tt(dve, t, t, x, ALU.mult, stage="newton"))
                steps.append(lambda to=(y if k < 2 else out): stt(to, t, 1.5, y, ALU.add, ALU.mult, stage="newton"))
            last = []

            def behind(step):
                dve.wait(*last)
                last[:] = [step()]
                if step is steps[-1]:
                    done.append(last[0])
            return [lambda step=step: behind(step) for step in steps]

        def norm_moments(src):
            for t in range(TILES):
                ev = dve.do(lambda e, t=t: e.bn_stats(stats[:, t, :], src[:, t, :]), "bn_stats")
            chained(ev)
            for t in range(TILES):
                ev = dve.do(lambda e, t=t: e.bn_aggr(moments[:, t, :], stats[:, t, :]), "bn_aggr")
            chained(ev)

        def norm_root(done):
            return root_steps(rstd[:, :], moments[:, :, 1], LN_EPS, ALU.add, nw_ln, done)

        def norm_apply(dst, src, r_ev, stage):
            dve.wait(r_ev)
            for t in range(TILES):
                ev = ts(dst[:, t, :], src[:, t, :], moments[:, t, 0:1], rstd[:, t:t + 1],
                        ALU.subtract, ALU.mult, stage=stage)
            return ev

        def layer_norm(dst, src, stage):
            norm_moments(src)
            done = []
            for step in norm_root(done):
                step()
            return norm_apply(dst, src, done[0], stage)

        def turn_tiles(src, events, stage):
            s = turned.take()
            pe.wait(*s.before, *events)
            for t in range(TILES):
                ev = turn(s.mem[:, t * P:(t + 1) * P], src(t), stage=stage if t == TILES - 1 else None)
            s.ready = ev
            return s

        def load_layer(l):
            w = wl.take()
            sp.wait(*w.before)
            w.ready = load(w.mem[:, :], io["wl"][l], f"weights{l % 2}")
            w.ready2 = load(cl[l % 2][:, :], io["cl"][l], f"columns{l % 2}")
            return w

        early = ExitStack()
        with early:
            def eb(name, shape, dt=F32):
                return sb(name, shape, dt, early)

            x0T = xT
            x0 = Ring([eb(f"x0_{i}", [P, TILES, D]) for i in range(2)])
            w_in = eb("w_in", [P, 2 * D])
            w_out = eb("w_out", [P, D])
            ccols = eb("ccols", [P, TAPS + 2])
            lnrow = eb("lnrow", [P, 2, D])
            rw = eb("rw", [P, EXPERTS])
            rrow = eb("rrow", [P, 2, EXPERTS])
            w1 = eb("w1", [P, EXPERTS, FF])
            w2 = eb("w2", [P, EXPERTS, FFC, D])
            b1 = eb("b1", [P, EXPERTS, FFC])
            b2 = eb("b2", [EXPERTS, D])
            wqkv = eb("wqkv", [P, (HQ + 2 * HKV) * DH])
            wo = eb("wo", [P, HQ, D])
            rope = eb("rope", [P, 2, TILES, DH])

            band32 = eb("band32", [P, 2, GROUP, KEYS])
            causal32 = eb("causal32", [P, P])
            load(band32[:, :, :, :], io["band"], "masks")
            masks_ev = load(causal32[:, :], io["causal"], "masks")
            act.wait(c_ev, masks_ev)
            copy(identb[:, :], ident[:, :], "masks")
            copy(band[:, :, :, :], band32[:, :, :, :], "masks")
            pe.wait(copy(causal[:, :], causal32[:, :], "masks"))

            io_ev = {}
            for dst, name in ((x0T, "x0T"), (w_in, "w_in"), (ccols, "ccols"), (w_out, "w_out"),
                              (lnrow, "lnrow"), (rw, "rw"), (rrow, "rrow"), (w1, "w1"), (b1, "b1"), (b2, "b2"),
                              (w2, "w2"), (wqkv, "wqkv"), (rope, "rope"), (wo, "wo")):
                full = dst[tuple(slice(None) for _ in dst.shape)]
                io_ev[name] = load(full, io[name], "load_" + name)

            gate = Ring([eb("gate0", [P, TOKENS])])
            val = Ring([eb("val0", [P, TOKENS + TAPS - 1])])
            y = Ring([eb("y0", [P, TOKENS])])
            resT = Ring([eb("resT0", [P, TOKENS])])
            x1 = Ring([eb(f"x1_{i}", [P, TILES, D]) for i in range(2)])
            x1T = Ring([eb(f"x1T{i}", [P, TOKENS]) for i in range(2)])
            x2T = Ring([eb(f"x2T{i}", [P, TOKENS]) for i in range(2)])
            conv = eb("conv", [P, TOKENS])
            tok = eb("tok", [P, TILES, D])
            tok2 = eb("tok2", [P, TILES, D])
            acc = eb("acc", [P, TILES, D])
            decay = eb("decay", [P, 1])
            lg = eb("lg", [P, TILES, EXPERTS])
            pr = eb("pr", [P, TILES, EXPERTS])
            rowst = eb("rowst", [P, 4, TILES])
            gates = eb("gates", [P, TILES, EXPERTS])
            gatesT = eb("gatesT", [EXPERTS, TOKENS])
            hbuf = Ring([eb(f"hbuf{i}", [P, FFC, TOKENS]) for i in range(2)])

            edge_ev = dve.do(lambda e: e.memset(val.slots[0].mem[:, :], 0.0), "edges")
            act.wait(io_ev["ccols"])
            decay_ev = activate(decay[:, :], ccols[:, TAPS + 1:TAPS + 2], ACT.Tanh, "decay")
            act.wait(edge_ev)
            dve.wait(decay_ev)

            def load_x0(b):
                s = x0.take()
                sp.wait(*s.before)
                s.ready = load(s.mem[:, :, :], io["x0"][b], f"x0_{b % 2}")
                return s

            x0_tok = {0: load_x0(0), 1: load_x0(1)}

            def per_tile(col):
                return col.unsqueeze(2).to_broadcast([P, TILES, EXPERTS])

            def tok_view(bank):
                return bank[:, :].rearrange("p (t d) -> p t d", t=TILES)

            def scan_block(b):
                sg, sv = proj.take(), proj.take()
                pe.wait(*sg.before, io_ev["x0T"], io_ev["w_in"])
                g_ev = mm(sg.mem[:, :], w_in[:, 0:D], x0T[:, b, :], stage="gate")
                pe.wait(*sv.before)
                v_ev = mm(sv.mem[:, :], w_in[:, D:2 * D], x0T[:, b, :], stage="val")
                gt, vl = gate.take(), val.take()
                act.wait(g_ev, *gt.before)
                sig_ev = activate(gt.mem[:, :], sg.mem[:, :], ACT.Sigmoid, "sigmoid")
                sg.free = [sig_ev]
                act.wait(v_ev, *vl.before)
                val_ev = copy(vl.mem[:, TAPS // 2:TAPS // 2 + TOKENS], sv.mem[:, :], "val")
                sv.free = [val_ev]
                yield
                dve.wait(val_ev, io_ev["ccols"])
                chained(ts(conv[:, :], vl.mem[:, 0:TOKENS], ccols[:, 0:1], ccols[:, TAPS:TAPS + 1],
                           ALU.mult, ALU.add, stage="conv"))
                for k in range(1, TAPS):
                    ev = chained(stt(conv[:, :], vl.mem[:, k:k + TOKENS], ccols[:, k:k + 1], conv[:, :],
                                     ALU.mult, ALU.add, stage="conv"))
                    if k % 2:
                        yield
                vl.free = [ev]
                dve.wait(sig_ev)
                ev = chained(tt(dve, conv[:, :], conv[:, :], gt.mem[:, :], ALU.mult, stage="conv"))
                gt.free = [ev]
                ys = y.take()
                dve.wait(*ys.before)
                scan_ev = dve.do(lambda e: e.tensor_tensor_scan(
                    ys.mem[:, :], decay[:, 0:1].to_broadcast([P, TOKENS]), conv[:, :], 0.0, ALU.mult, ALU.add), "scan")
                yield
                yield
                so = proj.take()
                pe.wait(*so.before, scan_ev, io_ev["w_out"])
                o_ev = mm(so.mem[:, :], w_out[:, :], ys.mem[:, :], stage="w_out")
                ys.free = [o_ev]
                rs = resT.take()
                dve.wait(o_ev, *rs.before, scan_ev)
                res_ev = tt(dve, rs.mem[:, :], so.mem[:, :], x0T[:, b, :], ALU.add, stage="res")
                so.free = [res_ev]
                yield
                s = turn_tiles(lambda t: rs.mem[:, t * P:(t + 1) * P], [res_ev], "res_tok")
                rs.free = [s.ready]
                dve.wait(s.ready)
                ln_ev = layer_norm(tok, tok_view(s.mem), "ln0")
                s.free = [ln_ev]
                yield
                dve.wait(ln_ev, io_ev["lnrow"], x0_tok[b].ready)
                chained(tt(dve, tok[:, :, :], tok[:, :, :], lnrow[:, 0:1, :].to_broadcast([P, TILES, D]),
                           ALU.mult, stage="affine"))
                chained(tt(dve, tok[:, :, :], tok[:, :, :], lnrow[:, 1:2, :].to_broadcast([P, TILES, D]),
                           ALU.add, stage="affine"))
                ev = chained(tt(dve, tok[:, :, :], tok[:, :, :], x0_tok[b].mem[:, :, :], ALU.add, stage="affine"))
                x0_tok[b].free = [ev]
                if b + 2 < SEQS:
                    x0_tok[b + 2] = load_x0(b + 2)
                yield
                x1s, x1Ts = x1.take(), x1T.take()
                dve.wait(*x1s.before)
                x1s.ready = layer_norm(x1s.mem, tok, "x1")
                yield
                yield
                s = turn_tiles(lambda t: x1s.mem[:, t, :], [x1s.ready], "x1T")
                act.wait(s.ready, *x1Ts.before)
                x1Ts.ready = copy(x1Ts.mem[:, :], s.mem[:, :], "x1T")
                s.free = [x1Ts.ready]
                x1_of[b] = x1s, x1Ts

            def experts(b):
                x1s, x1Ts = x1_of[b]
                s = proj.take()
                pe.wait(*s.before, x1Ts.ready, io_ev["rw"])
                for t in range(TILES):
                    ev = mm(s.mem[:, t * EXPERTS:(t + 1) * EXPERTS], x1Ts.mem[:, t * P:(t + 1) * P], rw[:, :],
                            stage="logits" if t == TILES - 1 else None)
                dve.wait(ev, io_ev["rrow"])
                ev = chained(tt(dve, lg[:, :, :], s.mem[:, 0:TILES * EXPERTS].rearrange("p (t e) -> p t e", t=TILES),
                                rrow[:, 0:1, :].to_broadcast([P, TILES, EXPERTS]), ALU.add, stage="router"))
                s.free = [ev]
                chained(reduce(rowst[:, 0, :], lg[:, :, :], ALU.max, stage="router"))
                ev = chained(tt(dve, lg[:, :, :], lg[:, :, :], per_tile(rowst[:, 0, :]), ALU.subtract, stage="router"))
                act.wait(ev)
                e_ev = activate(pr[:, :, :], lg[:, :, :], ACT.Exp, "router_exp")

                def route():
                    dve.wait(e_ev)
                    chained(reduce(rowst[:, 1, :], pr[:, :, :], ALU.add, stage="router"))
                    chained(recip(rowst[:, 2, :], rowst[:, 1, :], stage="router"))
                    chained(tt(dve, pr[:, :, :], pr[:, :, :], per_tile(rowst[:, 2, :]), ALU.mult, stage="router"))
                    chained(reduce(rowst[:, 0, :], pr[:, :, :], ALU.max, stage="router"))
                    chained(tt(dve, lg[:, :, :], pr[:, :, :], per_tile(rowst[:, 0, :]), ALU.is_equal, stage="router"))
                    chained(tt(dve, lg[:, :, :], lg[:, :, :], rrow[:, 1:2, :].to_broadcast([P, TILES, EXPERTS]),
                               ALU.mult, stage="router"))
                    chained(reduce(rowst[:, 3, :], lg[:, :, :], ALU.max, stage="router"))
                    chained(tt(dve, lg[:, :, :], lg[:, :, :], per_tile(rowst[:, 3, :]), ALU.is_equal, stage="router"))
                    return chained(tt(dve, gates[:, :, :], lg[:, :, :], pr[:, :, :], ALU.mult, stage="router"))

                def bias(g_ev):
                    s = turned.take()
                    pe.wait(*s.before, g_ev)
                    for t in range(TILES):
                        ev = turn(s.mem[0:EXPERTS, t * P:(t + 1) * P], gates[:, t, :],
                                  stage="gatesT" if t == TILES - 1 else None)
                    act.wait(ev)
                    gT_ev = copy(gatesT[:, :], s.mem[0:EXPERTS, :], "gatesT")
                    s.free = [gT_ev]
                    s = slow.take()
                    pe.wait(*s.before, gT_ev, io_ev["b2"])
                    for t in range(TILES):
                        ev = mm(s.mem[:, t * D:(t + 1) * D], gatesT[:, t * P:(t + 1) * P], b2[:, :],
                                stage="gate_b2" if t == TILES - 1 else None)
                    dve.wait(ev, x1s.ready)
                    ev = chained(tt(dve, acc[:, :, :], tok_view(s.mem), x1s.mem[:, :, :], ALU.add, stage="acc"))
                    s.free = [ev]
                    x1s.free = [ev]

                hid, dn = None, None
                for e_ in range(EXPERTS + 1):
                    prev = hid
                    if e_ < EXPERTS:
                        hid = hbuf.take()
                    for c in range(FFC):
                        if e_ < EXPERTS:
                            s = proj.take()
                            pe.wait(*s.before, x1Ts.ready, io_ev["w1"])
                            ev = mm(s.mem[:, :], w1[:, e_, c * P:(c + 1) * P], x1Ts.mem[:, :], stage="up")
                            act.wait(ev, *hid.before, io_ev["b1"])
                            hid.ready = activate(hid.mem[:, c, :], s.mem[:, :], ACT.Relu, "relu", bias=b1[:, e_, c:c + 1])
                            s.free = [hid.ready]
                            if e_ == EXPERTS - 1 and c == FFC - 1:
                                x1Ts.free = [ev]
                        if e_ == 0 and c == 0:
                            g_ev = route()
                        if e_ == 0 and c == 2:
                            bias(g_ev)
                        if e_ > 0:
                            if c == 0:
                                dn = slow.take()
                                pe.wait(*dn.before, prev.ready, io_ev["w2"])
                            for k in range(FFC):
                                ev = mm(dn.mem[:, c * D:(c + 1) * D], prev.mem[:, k, c * P:(c + 1) * P],
                                        w2[:, e_ - 1, k, :], start=k == 0, stop=k == FFC - 1,
                                        stage="down" if (c, k) == (TILES - 1, FFC - 1) else None)
                        yield
                    if e_ > 0:
                        prev.free = [ev]
                        dve.wait(ev)
                        for t in range(TILES):
                            ev = stt(acc[:, t, :], dn.mem[:, t * D:(t + 1) * D], gates[:, t, e_ - 1:e_], acc[:, t, :],
                                     ALU.mult, ALU.add, stage="acc")
                        dn.free = [ev]
                        dve.wait(ev)
                ln_ev = layer_norm(tok2, acc, "x2")
                yield
                x2s = x2T.take()
                s = turn_tiles(lambda t: tok2[:, t, :], [ln_ev], "x2T")
                dve.wait(s.ready)
                act.wait(s.ready, *x2s.before)
                x2s.ready = copy(x2s.mem[:, :], s.mem[:, :], "x2T")
                s.free = [x2s.ready]
                x2_of[b] = x2s

            prod = Ring([eb(f"prod{i}", [P, 2, GROUP, DH]) for i in range(2)])
            q2T = eb("q2T", [P, HQ, TOKENS])
            k2T = eb("k2T", [P, HKV, TOKENS])
            v2 = eb("v2", [P, TILES, HKV * DH])
            prob2 = Ring([eb(f"prob2{i}", [P, TOKENS]) for i in range(3)])
            prob2T = Ring([eb(f"prob2T{i}", [P, TILES, P]) for i in range(2)])
            soft2 = Ring([eb(f"soft2{i}", [P, 4]) for i in range(5)])
            o2 = Ring([eb("o2_0", [P, HQ, DH])])
            o2T = Ring([eb("o2T0", [P, HQ, P])])
            res2 = Ring([eb("res2_0", [P, TOKENS])])
            tok3 = eb("tok3", [P, TILES, D])
            scale2 = 1.0 / float(np.sqrt(np.float32(DH)))
            x1_of, x2_of, x3_ev, qkv_free = {}, {}, [None] * SEQS, []

            def attention(b):
                half = DH // 2
                x2s = x2_of[b]
                work, made = [(t, c) for t in range(TILES) for c in range(4)], {}
                for i in range(len(work) + 1):
                    if i < len(work):
                        t, c = work[i]
                        s = scores.take()
                        pe.wait(*s.before, x2s.ready, io_ev["wqkv"])
                        ev = mm(s.mem[:, :], x2s.mem[:, t * P:(t + 1) * P], wqkv[:, c * 512:(c + 1) * 512],
                                stage="qkv2")
                        if c == 3:
                            act.wait(ev, *qkv_free)
                            v_ev = copy(v2[:, t, :], s.mem[:, :], "v2")
                            s.free = [v_ev]
                        else:
                            w = prod.take()
                            made[t, c] = w
                            dve.wait(ev, *w.before, io_ev["rope"])
                            src = s.mem[:, :].rearrange("p (h d) -> p h d", h=GROUP)

                            def table2(k, lo, hi):
                                return rope[:, k, t, lo:hi].unsqueeze(1).to_broadcast([P, GROUP, hi - lo])
                            tt(dve, w.mem[:, 0, :, :], src, table2(0, 0, DH), ALU.mult)
                            tt(dve, w.mem[:, 1, :, 0:half], src[:, :, half:DH], table2(1, 0, half), ALU.mult)
                            w.ready = tt(dve, w.mem[:, 1, :, half:DH], src[:, :, 0:half], table2(1, half, DH),
                                         ALU.mult, stage="rope2")
                            s.free = [w.ready]
                    if i and work[i - 1][1] < 3:
                        t, c = work[i - 1]
                        w = made.pop((t, c))
                        z = turned.take()
                        pe.wait(*z.before, w.ready)
                        for j in range(GROUP):
                            turn(z.mem[:, j * P:(j + 1) * P], w.mem[:, 0, j, :], stop=False)
                            ev = turn(z.mem[:, j * P:(j + 1) * P], w.mem[:, 1, j, :], start=False,
                                      stage="rope2T" if j == GROUP - 1 else None)
                        w.free = [ev]
                        dst = (q2T[:, c * GROUP:(c + 1) * GROUP, t * P:(t + 1) * P] if c < 2
                               else k2T[:, :, t * P:(t + 1) * P])
                        act.wait(ev, *qkv_free)
                        qk_ev = copy(dst, z.mem[:, :].rearrange("p (j t) -> p j t", j=GROUP), "qk2T")
                        z.free = [qk_ev]
                    yield
                rs = res2.take()
                work = [(t, h) for t in range(TILES) for h in range(HQ)]
                kept = {}

                def score2_pe(t, h):
                    n = (t + 1) * P
                    s = scores.take()
                    pe.wait(*s.before, qk_ev)
                    mm(s.mem[:, 0:n], q2T[:, h, t * P:(t + 1) * P], k2T[:, h // 2, 0:n], stop=False)
                    s.ready = mm(s.mem[:, n - P:n], identb[:, :], causal[:, :], start=False, stage="score2")
                    m = soft2.take()
                    dve.wait(s.ready, *m.before)
                    chained(reduce(m.mem[:, 0:1], s.mem[:, 0:n], ALU.max, stage="max2"))
                    m.ready = ts(m.mem[:, 1:2], m.mem[:, 0:1], -scale2, None, ALU.mult, stage="max2")
                    kept[t, h] = (s, m)

                def exp2_act(t, h):
                    n = (t + 1) * P
                    s, m = kept[t, h]
                    p = prob2.take()
                    act.wait(m.ready, *p.before)
                    p.ready = activate(p.mem[:, 0:n], s.mem[:, 0:n], ACT.Exp, "exp2", scale=scale2,
                                       bias=m.mem[:, 1:2], accum_out=m.mem[:, 2:3])
                    s.free = [p.ready]
                    kept[t, h] = (m, p)

                def turn2(t, h):
                    m, p = kept[t, h]
                    z = turned.take()
                    pe.wait(*z.before, p.ready)
                    for k in range(t + 1):
                        ev = turn(z.mem[:, k * P:(k + 1) * P], p.mem[:, k * P:(k + 1) * P],
                                  stage="prob2T" if k == t else None)
                    p.free = [ev]
                    q = prob2T.take()
                    act.wait(ev, *q.before)
                    q.ready = copy(q.mem[:, 0:t + 1, :], z.mem[:, 0:(t + 1) * P].rearrange("p (k q) -> p k q", q=P),
                                   "prob2T")
                    z.free = [q.ready]
                    kept[t, h] = (m, p.ready, q)

                def weigh2(t, h):
                    m, e_ev, q = kept.pop((t, h))
                    o = summed.take()
                    pe.wait(*o.before, q.ready, v_ev)
                    for k in range(t + 1):
                        ev = mm(o.mem[:, 0:DH], q.mem[:, k, :], v2[:, k, (h // 2) * DH:(h // 2 + 1) * DH],
                                start=k == 0, stop=k == t, stage="pv2" if k == t else None)
                    q.free = [ev]
                    os = kept["o2"] = o2.take() if h == 0 else kept["o2"]
                    dve.wait(e_ev, *os.before)
                    chained(recip(m.mem[:, 3:4], m.mem[:, 2:3], stage="norm2"))
                    dve.wait(ev)
                    os.ready = ts(os.mem[:, h, :], o.mem[:, 0:DH], m.mem[:, 3:4], None, ALU.mult, stage="norm2")
                    o.free = [os.ready]
                    m.free = [os.ready]
                    if (t, h) == work[-1]:
                        qkv_free[:] = [ev]

                def turn_o2(t, g):
                    os, z = kept["o2"], turned.take()
                    d = kept["o2T"] = o2T.take() if g == 0 else kept["o2T"]
                    pe.wait(*z.before, os.ready)
                    for j in range(GROUP):
                        ev = turn(z.mem[:, j * P:(j + 1) * P], os.mem[:, g * GROUP + j, :],
                                  stage="o2T" if j == GROUP - 1 else None)
                    if g == 1:
                        os.free = [ev]
                    act.wait(ev, *d.before)
                    d.ready = copy(d.mem[:, g * GROUP:(g + 1) * GROUP, :],
                                   z.mem[:, :].rearrange("p (j t) -> p j t", j=GROUP), "o2T")
                    z.free = [d.ready]

                def project_o2(t):
                    d, s = kept["o2T"], summed.take()
                    pe.wait(*s.before, d.ready, io_ev["wo"])
                    for k in range(HQ):
                        ev = mm(s.mem[:, 0:P], wo[:, k, :], d.mem[:, k, :], start=k == 0, stop=k == HQ - 1,
                                stage="wo2" if k == HQ - 1 else None)
                    d.free = [ev]
                    dve.wait(ev, x2s.ready, *rs.before)
                    rs.ready = tt(dve, rs.mem[:, t * P:(t + 1) * P], s.mem[:, 0:P], x2s.mem[:, t * P:(t + 1) * P],
                                  ALU.add, stage="res2")
                    s.free = [rs.ready]

                for i in range(len(work) + 5):
                    if i < len(work):
                        score2_pe(*work[i])
                    if 1 <= i <= len(work):
                        exp2_act(*work[i - 1])
                    if i >= 3 and i - 3 < len(work):
                        weigh2(*work[i - 3])
                    if 2 <= i <= len(work) + 1:
                        turn2(*work[i - 2])
                    t, h = (i - 3) // HQ, (i - 3) % HQ
                    if h == HQ - 1 and 0 <= t < TILES:
                        turn_o2(t, 0)
                        turn_o2(t, 1)
                    if h == 0 and t > 0:
                        project_o2(t - 1)
                    yield
                x2s.free = [rs.ready]
                s = turn_tiles(lambda t: rs.mem[:, t * P:(t + 1) * P], [rs.ready], "res2_tok")
                rs.free = [s.ready]
                dve.wait(s.ready)
                ln_ev = layer_norm(tok3, tok_view(s.mem), "x3")
                s.free = [ln_ev]
                yield
                s = turn_tiles(lambda t: tok3[:, t, :], [ln_ev], "x3T")
                dve.wait(s.ready)
                act.wait(s.ready)
                copy(xT[:, b, :], s.mem[:, :], "x3T")
                x3_ev[b] = copy(x3T[:, b, :], s.mem[:, :], "x3T")
                s.free = [x3_ev[b]]

            layer_w = {0: load_layer(0)}
            attention_steps = TILES * (4 + HQ) + 6
            parts = [{"run": attention, "rate": 1.0, "before": 1, "behind": None},
                     {"run": experts, "rate": 1.1 * (EXPERTS * FFC + 5) / attention_steps, "before": 2, "behind": 0},
                     {"run": scan_block, "rate": 1.1 * 13 / attention_steps, "before": None, "behind": 1}]
            for part in parts:
                part.update(done=0, thread=None, credit=0.0)
            while parts[0]["done"] < SEQS:
                for part in parts:
                    b = part["done"]
                    before, behind = part["before"], part["behind"]
                    if part["thread"] is None:
                        if (b == SEQS or (before is not None and parts[before]["done"] <= b)
                                or (behind is not None and parts[behind]["done"] < b - 1)):
                            continue
                        part["thread"], part["credit"] = part["run"](b), 0.0
                    alone = not any(other["thread"] for other in parts[:parts.index(part)])
                    part["credit"] = max(part["credit"] + part["rate"], 1.0 if alone else 0.0)
                    while part["credit"] >= 1.0 and part["thread"]:
                        part["credit"] -= 1.0
                        if next(part["thread"], "end") == "end":
                            part["thread"], part["done"] = None, b + 1

        ends = []
        for src in (pe, act, dve):
            ends += [Event(src.sems[k], src.counts[k]) for k in src.sems]
        for lane in (pe, act, dve, pool, sp):
            lane.wait(*ends)

        wl.slots.append(Slot(sb("wl1", [P, W_ALL])))
        wl.at = 1
        base = sb("base", [P, 4, TILES, DL])
        table = sb("table", [P, 4, TILES, DL])
        qkrow = [sb(f"qkrow{i}", [P, 4, DL]) for i in range(2)]
        base_ev = load(base[:, :, :, :], io["base"], "base")

        xs = Ring([sb(f"xs{i}", [P, TOKENS]) for i in range(2)])
        xf = Ring([sb("xf0", [P, TOKENS])])
        raw = Ring([sb(f"raw{i}", [P, 8, DL]) for i in range(8)])
        sq = Ring([sb(f"sq{i}", [P, 8, DL]) for i in range(2)])
        rot = Ring([sb(f"rot{i}", [P, 8, DL]) for i in range(3)])
        n2 = Ring([sb(f"n2{i}", [P, 2 * HEADS]) for i in range(2)])
        rn = Ring([sb(f"rn{i}", [P, 2 * HEADS]) for i in range(2)])
        qT = Ring([sb(f"qT{i}", [P, PAIRS, P]) for i in range(2)])
        kT = Ring([sb(f"kT{i}", [P, PAIRS, WINDOW + P]) for i in range(3)])
        vs = Ring([sb(f"vs{i}", [P, HEADS // 2, DL + 1]) for i in range(2)])
        vp = Ring([sb(f"vp{i}", [KEYS, PACKS, HEADS, DL + 1]) for i in range(3)])
        soft = Ring([sb(f"soft{i}", [P, 2, GROUP]) for i in range(4)])
        prob = Ring([sb(f"prob{i}", [P, GROUP, KEYS]) for i in range(3)])
        probT = Ring([sb(f"probT{i}", [KEYS, GROUP, P]) for i in range(2)])
        ot = Ring([sb(f"ot{i}", [P, HEADS, DL]) for i in range(2)])
        oT = Ring([sb("oT0", [P, PAIRS, TOKENS])])
        xn = sb("xn", [P, TILES, D])
        xnT = sb("xnT", [P, TOKENS])
        glu = Ring([sb(f"glu{i}", [P, TOKENS]) for i in range(2)])
        hT = Ring([sb("hT0", [P, GLUC, TOKENS])])

        TOTAL = DEPTH * SEQS * TILES
        GROUPS = HEADS // GROUP
        x_ev = list(x3_ev)
        xs_of, tab_ev, tab_free = {}, {}, {0: [], 1: [], "last": []}
        state = {}
        batch = {}
        out_ev = []

        def where(n):
            return n // (SEQS * TILES), n // TILES % SEQS, n % TILES

        last_pool = [None]

        def on_pool(build_, stage):
            pool.wait(last_pool[0])
            last_pool[0] = pool.do(build_, stage)
            return last_pool[0]

        def unit(x, inverse):
            return on_pool(lambda e: e.tensor_tensor(x, x, inverse, ALU.mult), "unit")

        def shifted(dst, b, name):
            load(dst[0:D // 2, :], xT[0:D // 2, b, :], name)
            return load(dst[D // 2:D, 1:TOKENS], xT[D // 2:D, b, 0:TOKENS - 1], name)

        def shift_ahead(l, b):
            if l < DEPTH:
                s = xs.take()
                sp.wait(*s.before, x_ev[b])
                s.ready = shifted(s.mem, b, f"xs{b % 2}")
                xs_of[l, b] = s

        between = []

        def fill():
            for chain in between:
                chain.pop(0)()
            between[:] = [c for c in between if c]

        for s in xs.slots:
            ones_ev = on_pool(lambda e, s=s: e.memset(s.mem[:, 0:1], 0.0), "fill")
        for s in vs.slots:
            ones_ev = on_pool(lambda e, s=s: e.memset(s.mem[:, :, DL:DL + 1], 1.0), "fill")
        pe.wait(ones_ev)
        act.wait(ones_ev)
        sp.wait(ones_ev)
        shift_ahead(0, 0)

        def tables(l):
            row = qkrow[l % 2]
            sp.wait(*tab_free[l % 2])
            r_ev = load(row[:, :, :], io["qkrow"][l], f"qkrow{l % 2}")
            dve.wait(r_ev, base_ev, *tab_free["last"])
            for k in range(4):
                ev = tt(dve, table[:, k, :, :], base[:, k, :, :],
                        row[:, k:k + 1, :].to_broadcast([P, TILES, DL]), ALU.mult, stage="tables")
            tab_ev[l] = ev

        def qk_pe(n, part):
            l, b, t = where(n)
            if part == 0:
                if t == TILES // 2:
                    shift_ahead(*where(n + TILES)[:2])
                state[n] = {"raw": [], "n2": n2.take()}
            s, w = xs_of[l, b], layer_w[l]
            bank = proj.take()
            pe.wait(*bank.before, s.ready, w.ready)
            bank.ready = mm(bank.mem[:, :], s.mem[:, t * P:(t + 1) * P],
                            w.mem[:, part * 512:(part + 1) * 512], stage="qk")
            state[n]["qk", part] = bank

        def qk_act(n, part):
            st = state[n]
            bank, q, r = st.pop(("qk", part)), sq.take(), raw.take()
            src = bank.mem[:, :].rearrange("p (h d) -> p h d", d=DL)
            act.wait(bank.ready, *q.before, *r.before)
            q.ready = activate(q.mem[:, :, :], src, ACT.Square, "square")
            r.ready = copy(r.mem[:, :, :], src, "raw")
            bank.free = [r.ready]
            st["sq", part] = q
            st["raw"].append(r)

        def norm_dve(n, part):
            st = state[n]
            q = st.pop(("sq", part))
            dve.wait(q.ready, *st["n2"].before)
            n_ev = reduce(st["n2"].mem[:, part * 8:(part + 1) * 8], q.mem[:, :, :], ALU.add, stage="norm2sum")
            q.free = [n_ev]
            if part == 3:
                st["rn"] = rn.take()
                dve.wait(n_ev, *st["rn"].before)
                st["root"] = []
                between.append(root_steps(st["rn"].mem[:, :], st["n2"].mem[:, :], 1e-24, ALU.max, nw, st["root"]))

        def unit_pool(n, part):
            st = state[n]
            r, inv = st["raw"][part], st["rn"]
            while not st["root"]:
                fill()
            if part == 0:
                st["n2"].free = [st["root"][0]]
            pool.wait(st["root"][0], r.ready)
            r.ready = unit(r.mem[:, :, :], inv.mem[:, part * 8:(part + 1) * 8].unsqueeze(2).to_broadcast([P, 8, DL]))
            if part == 3:
                inv.free = [r.ready]

        def v_pe(n, half):
            l, b, t = where(n)
            st, s, w = state[n], xs_of[l, b], layer_w[l]
            bank = proj.take()
            pe.wait(*bank.before, s.ready, w.ready)
            bank.ready = mm(bank.mem[:, :], s.mem[:, t * P:(t + 1) * P],
                            w.mem[:, 2 * INNER + half * 512:2 * INNER + (half + 1) * 512], stage="v")
            st["v", half] = bank
            if t == TILES - 1 and half == 1:
                s.free = [bank.ready]

        def v_act(n, half):
            bank, v = state[n].pop(("v", half)), vs.take()
            act.wait(bank.ready, *v.before)
            v.ready = copy(v.mem[:, :, 0:DL], bank.mem[:, :].rearrange("p (h d) -> p h d", d=DL), "v")
            bank.free = [v.ready]
            state[n]["vs", half] = v

        def v_dma(n, half):
            l, b, t = where(n)
            st, hs = state[n], slice(half * 8, (half + 1) * 8)
            if half == 0:
                st["vp"] = vp.take()
                st["vp"].ready = []
                if t == 0:
                    pool.wait(*st["vp"].before)
                    st["vp"].edge = on_pool(lambda e, v=st["vp"]: e.memset(v.mem[0:WINDOW, 0, :, :], 0.0), "vp_edge")
            v, d = st.pop(("vs", half)), st["vp"]
            sp.wait(v.ready, *d.before)
            load(d.mem[WINDOW:KEYS, 0, hs, :], v.mem[0:PACK, :, :], f"v{half}")
            ev = load(d.mem[:, 1, hs, :], v.mem[P - KEYS:P, :, :], f"v{half}")
            v.free = [ev]
            d.ready.append(ev)

        def v_edge(n):
            if where(n)[2] < TILES - 1:
                d, nxt = state[n]["vp"], vp.slots[vp.at % len(vp.slots)]
                sp.wait(*d.ready, *nxt.free)
                nxt.edge = load(nxt.mem[0:WINDOW, 0, :, :], d.mem[PACK:KEYS, 1, :, :],
                                f"v_edge{vp.at % len(vp.slots)}")
                state[n]["v_moved"] = nxt.edge

        def rotate_dve(n, part):
            l, b, t = where(n)
            st = state[n]
            if part == 0:
                if n % (SEQS * TILES) == 0:
                    tables(l)
                    if l == 0:
                        layer_w[1] = load_layer(1)
            r, v = st["raw"][part], rot.take()
            which = 0 if part < 2 else 2
            half = DL // 2

            def tab(k, lo, hi):
                return table[:, k, t, lo:hi].unsqueeze(1).to_broadcast([P, 8, hi - lo])
            dve.wait(r.ready, tab_ev[l], *v.before)
            tt(dve, v.mem[:, :, 0:half], r.mem[:, :, half:DL], tab(which + 1, 0, half), ALU.mult)
            ev = tt(dve, v.mem[:, :, half:DL], r.mem[:, :, 0:half], tab(which + 1, half, DL), ALU.mult,
                    stage="rot_sin")
            fill()
            dve.wait(ev)
            v.ready = tt(dve, r.mem[:, :, :], r.mem[:, :, :], tab(which, 0, DL), ALU.mult, stage="rot_cos")
            if n % (SEQS * TILES) == SEQS * TILES - 1:
                tab_free.update({l % 2: [v.ready], "last": [v.ready]})
            st["rot", part] = v

        def rotate_pool(n, part):
            v, r = state[n]["rot", part], state[n]["raw"][part]
            pool.wait(v.ready)
            v.ready = on_pool(lambda e: e.tensor_tensor(v.mem[:, :, :], v.mem[:, :, :], r.mem[:, :, :], ALU.add), "rot")
            r.free = [v.ready]

        def rotate_pe(n, part):
            st = state[n]
            v, z = st.pop(("rot", part)), turned.take()
            pe.wait(*z.before, v.ready)
            for j in range(4):
                ev = turn(z.mem[:, j * P:(j + 1) * P], v.mem[:, 2 * j:2 * j + 2, :], stage="qkT" if j == 3 else None)
            z.ready, v.free = ev, [ev]
            st["qkT", part] = z

        def rotate_act(n, part):
            l, b, t = where(n)
            st = state[n]
            if part == 0:
                st["qT"], st["kT"] = qT.take(), kT.take()
                k = st["kT"]
                if t == 0:
                    pool.wait(*k.before)
                    k.edge = on_pool(lambda e: e.memset(k.mem[:, :, 0:WINDOW], 0.0), "kT_edge")
            z = st.pop(("qkT", part))
            ps = slice((part % 2) * 4, (part % 2) * 4 + 4)
            src = z.mem[:, :].rearrange("p (j t) -> p j t", j=4)
            if part < 2:
                q = st["qT"]
                act.wait(z.ready, *q.before)
                q.ready = copy(q.mem[:, ps, :], src, "qT")
                z.free = [q.ready]
            else:
                k = st["kT"]
                act.wait(z.ready, *k.before)
                k.ready = copy(k.mem[:, ps, WINDOW:WINDOW + P], src, "kT")
                z.free = [k.ready]
            if part == 3 and t < TILES - 1:
                nxt = kT.slots[kT.at % len(kT.slots)]
                k = st["kT"]
                pool.wait(k.ready, *nxt.free)
                nxt.edge = on_pool(lambda e: e.tensor_copy(nxt.mem[:, :, 0:WINDOW], k.mem[:, :, P:P + WINDOW]),
                                   "kT_edge")
                st["edge_copied"] = nxt.edge

        def heads_of(g):
            return g % 2, 4 * (g // 2)

        def score_pe(n, g):
            l, b, t = where(n)
            st = state[n]
            q, k = st["qT"], st["kT"]
            parity, first = heads_of(g)
            s = scores.take()
            pe.wait(*s.before, q.ready, k.ready, k.edge)
            mm(s.mem[:, 0:GROUP * KEYS], identb[:, :], band[:, 1 if t == 0 else 0, :, :], stop=False)
            rows = slice(parity * DL, (parity + 1) * DL)
            for j in range(GROUP):
                for a in range(PACKS):
                    ev = mm(s.mem[a * PACK:(a + 1) * PACK, j * KEYS:(j + 1) * KEYS],
                            q.mem[rows, first + j, a * PACK:(a + 1) * PACK],
                            k.mem[rows, first + j, a * PACK:a * PACK + KEYS], start=False,
                            stage="score" if (j, a) == (GROUP - 1, PACKS - 1) else None)
            if g == GROUPS - 1:
                q.free, k.free = [ev], [ev, st.get("edge_copied")]
            s.ready = ev
            st["score", g] = s

        def soft_dve(n, g):
            st = state[n]
            s, m, p = st.pop(("score", g)), soft.take(), prob.take()
            view = s.mem[:, 0:GROUP * KEYS].rearrange("p (j k) -> p j k", j=GROUP)
            dve.wait(s.ready, *m.before, *p.before)
            ev = reduce(m.mem[:, 0, :], view, ALU.max, stage="max")
            fill()
            dve.wait(ev)
            p.ready = tt(dve, p.mem[:, :, :], view, m.mem[:, 0, :].unsqueeze(2).to_broadcast([P, GROUP, KEYS]),
                         ALU.subtract, stage="less_max")
            s.free = [p.ready]
            st["soft", g] = (m, p)

        def exp_act(n, g):
            m, p = state[n]["soft", g]
            act.wait(p.ready)
            p.ready = activate(p.mem[:, :, :], p.mem[:, :, :], ACT.Exp, "exp", scale=QK_SCALE)

        def prob_pe(n, g):
            st = state[n]
            m, p = st["soft", g]
            z = turned.take()
            pe.wait(*z.before, p.ready)
            for j in range(GROUP):
                ev = turn(z.mem[0:KEYS, j * P:(j + 1) * P], p.mem[:, j, :], stage="probT" if j == GROUP - 1 else None)
            p.free, z.ready = [ev], ev
            st["probT", g] = z

        def prob_act(n, g):
            st = state[n]
            z, pt = st.pop(("probT", g)), probT.take()
            act.wait(z.ready, *pt.before)
            pt.ready = copy(pt.mem[:, :, :], z.mem[0:KEYS, :].rearrange("p (j q) -> p j q", j=GROUP), "probT")
            z.free = [pt.ready]
            st["pt", g] = pt

        def weigh_pe(n, g):
            st = state[n]
            pt, v = st.pop(("pt", g)), st["vp"]
            parity, first = heads_of(g)
            s = summed.take()
            pe.wait(*s.before, pt.ready, *v.ready, v.edge)
            for j in range(GROUP):
                head = 2 * (first + j) + parity
                for a in range(PACKS):
                    ev = mm(s.mem[a * PACK:(a + 1) * PACK, j * (DL + 1):(j + 1) * (DL + 1)],
                            pt.mem[:, j, a * PACK:(a + 1) * PACK], v.mem[:, a, head, :],
                            stage="weigh" if (j, a) == (GROUP - 1, PACKS - 1) else None)
            pt.free, s.ready = [ev], ev
            st["sum", g] = s
            if g == GROUPS - 1:
                v.free = [ev, st.get("v_moved")]

        def divide_dve(n, g):
            st = state[n]
            s, (m, p) = st.pop(("sum", g)), st.pop(("soft", g))
            parity, first = heads_of(g)
            if g == 0:
                st["ot"] = ot.take()
            o = st["ot"]
            view = s.mem[:, 0:GROUP * (DL + 1)].rearrange("p (j d) -> p j d", j=GROUP)
            dve.wait(s.ready, *o.before)
            ev = recip(m.mem[:, 1, :], view[:, :, DL], stage="recip")
            fill()
            dve.wait(ev)
            dst = o.mem[:, :, :].rearrange("p (pair two) d -> p two pair d", two=2)[:, parity, first:first + GROUP, :]
            o.ready = tt(dve, dst, view[:, :, 0:DL],
                         m.mem[:, 1, :].unsqueeze(2).to_broadcast([P, GROUP, DL]), ALU.mult, stage="o")
            s.free, m.free = [o.ready], [o.ready]

        def out_pe(n, part):
            o = state[n]["ot"]
            z = turned.take()
            pe.wait(*z.before, o.ready)
            for j in range(4):
                two = slice(part * 8 + 2 * j, part * 8 + 2 * j + 2)
                ev = turn(z.mem[:, j * P:(j + 1) * P], o.mem[:, two, :], stage="oT" if j == 3 else None)
            z.ready = ev
            state[n]["oT", part] = z
            if part == 1:
                o.free = [ev]

        def out_act(n, part):
            l, b, t = where(n)
            if t == 0 and part == 0:
                batch[l, b] = {"oT": oT.take()}
            d, z = batch[l, b]["oT"], state[n].pop(("oT", part))
            act.wait(z.ready, *d.before)
            d.ready = copy(d.mem[:, part * 4:part * 4 + 4, t * P:(t + 1) * P],
                           z.mem[:, :].rearrange("p (j t) -> p j t", j=4), "oT")
            z.free = [d.ready]

        def finish(l, b):
            w, col = layer_w[l], cl[l % 2]
            d = batch[l, b]["oT"]

            def columns(lo, n=1):
                return col[:, lo:lo + n]

            def turn_slow(src, events, stage):
                z = slow.take()
                pe.wait(*z.before, *events)
                for t in range(TILES):
                    z.ready = turn(z.mem[:, t * P:(t + 1) * P], src(t), stage=stage if t == TILES - 1 else None)
                return z
            s = slow.take()
            pe.wait(*s.before, d.ready)
            for j in range(PAIRS):
                ev = mm(s.mem[:, :], w.mem[:, W_O + j * D:W_O + (j + 1) * D], d.mem[:, j, :], start=j == 0,
                        stop=j == PAIRS - 1, stage="wo" if j == PAIRS - 1 else None)
                if j == PAIRS // 2 - 1:
                    yield
            d.free = [ev]
            yield
            dve.wait(ev, xs_of[l, b].ready)
            r_ev = tt(dve, xT[:, b, :], s.mem[:, :], xT[:, b, :], ALU.add, stage="res")
            s.free = [r_ev]
            f = xf.take()
            pool.wait(*f.before)
            sp.wait(on_pool(lambda e: e.memset(f.mem[D // 2:D, 0:1], 0.0), "xf"), r_ev, *f.before)
            f_ev = shifted(f.mem, b, "xf")
            yield
            z = turn_slow(lambda t: f.mem[:, t * P:(t + 1) * P], [f_ev], "xf_tok")
            f.free = [z.ready]
            yield
            dve.wait(z.ready)
            view = z.mem[:, :].rearrange("p (t d) -> p t d", t=TILES)
            norm_moments(view)
            done = []
            between.append(norm_root(done))
            while not done:
                yield
            n_ev = norm_apply(xn, view, done[0], "xn")
            z.free = [n_ev]
            yield
            z = turn_slow(lambda t: xn[:, t, :], [n_ev], "xnT")
            dve.wait(z.ready)
            act.wait(z.ready, w.ready2)
            xn_ev = activate(xnT[:, :], z.mem[:, :], ACT.Identity, "xnT", scale=columns(C_G), bias=columns(C_B))
            z.free = [xn_ev]
            h = hT.take()
            for c in range(GLUC):
                yield
                s = proj.take()
                pe.wait(*s.before, xn_ev)
                ev = mm(s.mem[:, :], w.mem[:, W_1 + GLUP + c * P:W_1 + GLUP + (c + 1) * P], xnT[:, :], stage="w1")
                g = glu.take()
                act.wait(ev, *g.before)
                g_ev = activate(g.mem[:, :], s.mem[:, :], ACT.Gelu, "gelu", bias=columns(C_B1 + GLUC + c))
                s.free = [g_ev]
                s = slow.take()
                pe.wait(*s.before)
                ev = mm(s.mem[:, :], w.mem[:, W_1 + c * P:W_1 + (c + 1) * P], xnT[:, :], stage="w1")
                dve.wait(ev, g_ev, *h.before)
                h_ev = stt(h.mem[:, c, :], s.mem[:, :], columns(C_B1 + c), g.mem[:, :], ALU.add, ALU.mult, stage="hT")
                s.free = [h_ev]
                g.free = [h_ev]
            act.wait(ev)
            yield
            s = slow.take()
            pe.wait(*s.before, h_ev)
            for c in range(GLUC):
                ev = mm(s.mem[:, :], w.mem[:, W_2 + c * D:W_2 + (c + 1) * D], h.mem[:, c, :], start=c == 0,
                        stop=c == GLUC - 1, stage="w2" if c == GLUC - 1 else None)
            h.free = [ev]
            yield
            dve.wait(ev, f_ev)
            x_ev[b] = stt(xT[:, b, :], s.mem[:, :], columns(C_B2), xT[:, b, :], ALU.add, ALU.add, stage="x")
            s.free = [x_ev[b]]
            dve.wait(x_ev[b])
            if b == SEQS - 1:
                w.free = [ev, x_ev[b]]
                if l + 2 < DEPTH:
                    layer_w[l + 2] = load_layer(l + 2)
            if l == DEPTH - 1:
                yield
                f = xf.take()
                dve.wait(*f.before)
                a_ev = tt(dve, f.mem[:, :], xT[:, b, :], x3T[:, b, :], ALU.add, stage="last_sum")
                yield
                z = turn_slow(lambda t: f.mem[:, t * P:(t + 1) * P], [a_ev], "last_tok")
                yield
                dve.wait(z.ready)
                last = f.mem[:, :].rearrange("p (t d) -> p t d", t=TILES)
                n_ev = layer_norm(last, z.mem[:, :].rearrange("p (t d) -> p t d", t=TILES), "last_ln")
                z.free = [n_ev]
                sp.wait(n_ev)
                f.free = [load(io["out"][b].rearrange("(t p) d -> p t d", p=P), last, "store")]
                out_ev[:] = f.free

        pending = []
        QUARTERS = TOTAL * GROUPS
        AHEAD, ROT, VAL = 12, 5, GROUPS

        def at(stage, i):
            if 0 <= i < QUARTERS:
                stage(i // GROUPS, i % GROUPS)

        for G in range(-AHEAD, QUARTERS + 12):
            at(score_pe, G)
            at(exp_act, G - 1)
            i = G - 6
            if i >= 0 and i % GROUPS < 2 and i < QUARTERS:
                at(out_pe, i)
                at(out_act, i)
                n = i // GROUPS
                if i % GROUPS == 1:
                    state.pop(n, None)
                    if where(n)[2] == TILES - 1:
                        pending.append(finish(*where(n)[:2]))
            at(qk_pe, G + AHEAD)
            at(norm_dve, G + AHEAD - 1)
            at(unit_pool, G + ROT + 1)
            at(rotate_dve, G + ROT)
            fill()
            at(rotate_pool, G + ROT)
            at(soft_dve, G)
            fill()
            at(qk_act, G + AHEAD)
            i = G + VAL
            if 0 <= i < QUARTERS:
                if i % GROUPS < 2:
                    at(v_pe, i)
                    at(v_act, i)
                    at(v_dma, i)
                elif i % GROUPS == 3:
                    v_edge(i // GROUPS)
            at(rotate_pe, G + ROT - 1)
            at(rotate_act, G + ROT - 1)
            at(weigh_pe, G - 2)
            at(divide_dve, G - 2)
            fill()
            at(prob_pe, G - 1)
            at(prob_act, G - 1)
            if pending and next(pending[0], "end") == "end":
                pending.pop(0)
            fill()
        while pending:
            fill()
            if next(pending[0], "end") == "end":
                pending.pop(0)
        sp.wait(*out_ev)

        block = ctx.enter_context(nc.Block())

        @block.sync
        def _(e):
            sp.play(e)

        @block.tensor
        def _(e):
            pe.play(e)

        @block.scalar
        def _(e):
            act.play(e)

        @block.vector
        def _(e):
            dve.play(e)

        @block.gpsimd
        def _(e):
            pool.play(e)


def shape_constants():
    f = np.float32
    c = {"ident": np.eye(P, dtype=f)}
    i = np.arange(P)
    c["causal"] = np.where(i[None, :] > i[:, None], f(MASKED), f(0))
    q, k = i % PACK, np.arange(KEYS)
    ok = (k[None, :] >= q[:, None]) & (k[None, :] <= q[:, None] + WINDOW)
    ok0 = ok & ~((i[:, None] < PACK) & (k[None, :] < WINDOW))
    band = np.stack([ok, ok0], 1)[:, :, None, :].repeat(GROUP, 2)
    c["band"] = np.where(band, f(0), f(MASKED))

    def tiles(a):
        return np.ascontiguousarray(a.reshape(TILES, P, -1).transpose(1, 0, 2))
    t = np.arange(TOKENS, dtype=f)
    inv = f(1.0) / np.power(f(10000.0), np.arange(0, DH, 2, dtype=f) / f(DH))
    fr = np.concatenate([t[:, None] * inv] * 2, 1).astype(f)
    sgn = np.where(np.arange(DH) < DH // 2, f(-1), f(1))
    c["rope"] = np.stack([tiles(np.cos(fr)), tiles(np.sin(fr) * sgn)], 1)
    half = np.arange(0, DL, 2, dtype=f)
    inv = f(1.0) / np.power(f(10000.0), half / f(DL))
    fr = np.concatenate([t[:, None] * inv] * 2, 1).astype(f)
    bs = (half + f(0.4 * DL)) / f(1.4 * DL)
    power = (t - f(TOKENS // 2)) / f(WINDOW // 2)
    s = np.power(bs[None, :], power[:, None]).astype(f)
    s = np.concatenate([s, s], 1)
    sgn = np.where(np.arange(DL) < DL // 2, f(-1), f(1))
    r = f(1.0) / s
    c["base"] = np.stack([tiles(np.cos(fr) * s), tiles(np.sin(fr) * sgn * s),
                          tiles(np.cos(fr) * r), tiles(np.sin(fr) * sgn * r)], 1)
    return {k: np.ascontiguousarray(v) for k, v in c.items()}


def kernel(**inputs):
    import concourse.bacc as _bacc
    from concourse.bass_utils import run_bass_kernel_spmd as _run

    g = {k: np.asarray(v) for k, v in inputs.items()}
    a = shape_constants()
    x = g["L0_attn_x"]

    def rows(v):
        return np.broadcast_to(v[None], (P,) + v.shape)

    def padded(v, axis, n):
        shape = list(v.shape)
        shape[axis] = n - shape[axis]
        return np.concatenate([v, np.zeros(shape, v.dtype)], axis)

    a["x0T"] = x.transpose(2, 0, 1)
    a["x0"] = x.reshape(SEQS, TILES, P, D).transpose(0, 2, 1, 3)
    a["w_in"] = g["L0_attn_W_in"].T
    a["w_out"] = g["L0_attn_W_out"].T
    a["ccols"] = np.concatenate([g["L0_attn_conv_w"][:, 0, :], g["L0_attn_conv_b"][:, None],
                                 g["L0_attn_a_param"][:, None]], 1)
    a["lnrow"] = rows(np.stack([g["L0_attn_ln_w"], g["L0_attn_ln_b"]]))
    a["rw"] = g["L0_ffn_router_W"]
    a["rrow"] = rows(np.stack([g["L0_ffn_router_b"], np.arange(EXPERTS, 0, -1, dtype=np.float32)]))
    a["w1"] = g["L0_ffn_W1"].transpose(1, 0, 2)
    a["w2"] = g["L0_ffn_W2"].reshape(EXPERTS, FFC, P, D).transpose(2, 0, 1, 3)
    a["b1"] = g["L0_ffn_b1"].reshape(EXPERTS, FFC, P).transpose(2, 0, 1)
    a["b2"] = g["L0_ffn_b2"]
    a["wqkv"] = np.concatenate([g["L1_attn_Wq"], g["L1_attn_Wk"], g["L1_attn_Wv"]], 1)
    a["wo"] = g["L1_attn_Wo"].reshape(HQ, DH, D).transpose(1, 0, 2)
    w1 = g["L1_ffn_W1"]
    b1 = g["L1_ffn_b1"]
    wo = g["L1_ffn_Wo"].reshape(DEPTH, PAIRS, P, D).transpose(0, 2, 1, 3).reshape(DEPTH, P, PAIRS * D)
    w2 = padded(g["L1_ffn_W2"], 1, GLUP).reshape(DEPTH, GLUC, P, D).transpose(0, 2, 1, 3).reshape(DEPTH, P, GLUC * D)
    a["wl"] = np.concatenate([g["L1_ffn_Wqkv"], wo, padded(w1[:, :, :GLU], 2, GLUP),
                              padded(w1[:, :, GLU:], 2, GLUP), w2], 2)
    cols = np.concatenate([padded(b1[:, :GLU], 1, GLUP), padded(b1[:, GLU:], 1, GLUP)], 1)
    a["cl"] = np.concatenate([g["L1_ffn_ln_g"][:, :, None], g["L1_ffn_ln_b"][:, :, None],
                              g["L1_ffn_b2"][:, :, None],
                              cols.reshape(DEPTH, 2 * GLUC, P).transpose(0, 2, 1)], 2)
    half = DL // 2
    qs, ks = g["L1_ffn_q_scale"], g["L1_ffn_k_scale"]

    def swap(v):
        return np.concatenate([v[:, half:], v[:, :half]], 1)
    row = np.stack([qs, swap(qs), ks, swap(ks)], 1)
    a["qkrow"] = np.broadcast_to(row[:, None], (DEPTH, P) + row.shape[1:])

    nc = _bacc.Bacc("TRN2", target_bir_lowering=False, num_devices=1)
    arrays, io = {}, {}
    for name, v in a.items():
        v = np.ascontiguousarray(v)
        arrays[f"in_{name}"] = v
        ap = nc.dram_tensor(f"in_{name}", v.shape, mybir.dt.from_np(v.dtype), kind="ExternalInput").ap()
        io[name] = ap
    io["out"] = nc.dram_tensor("out_0", (SEQS, TOKENS, D), F32, kind="ExternalOutput").ap()
    build(nc, io)
    r = _run(nc, [arrays], core_ids=[0])
    return r.results[0]["out_0"]
```
